# Optimizing a Trainium2 kernel written in Bass

```python
import numpy as np
import jax
import jax.numpy as jnp

def _softmax(x, axis=-1):
    return jax.nn.softmax(x, axis=axis)

def _gelu(x):
    return jax.nn.gelu(x, approximate=True)

def _silu(x):
    return jax.nn.silu(x)

def _sigmoid(x):
    return jax.nn.sigmoid(x)

def _layernorm(x, axis=-1, eps=1e-05):
    m = jnp.mean(x, axis=axis, keepdims=True)
    v = jnp.var(x, axis=axis, keepdims=True)
    return (x - m) / jnp.sqrt(v + eps)

def _scatter_add(tgt, idx, src, axis=0):
    return tgt.at[idx].add(src)

def _segment_sum(src, seg, n):
    return jax.ops.segment_sum(src, seg, n)
kernel_name = 'mk_seq_preln_d1_jaxref_r4_f59a8b'

def setup_inputs(seed: int=0):
    np.random.seed(seed)
    _w = jnp.asarray

    def _L0_attn_setup():
        import jax, jax.numpy as jnp
        import numpy as np
        from jax import lax
        BLOCK_LEN = 128
        NEG_INF = -1000000000.0
        key = jax.random.key(seed)
        ks = jax.random.split(key, 8)
        N, L, Dm = (2, 2048, 1024)
        W, H, dh = (256, 16, 64)
        s = lambda fan: 1.0 / np.sqrt(fan)
        return {'inputs': jax.random.normal(ks[0], (N, L, Dm), jnp.float32), 'conv_w': jax.random.normal(ks[1], (3, Dm, 3 * W), jnp.float32) * s(3 * Dm), 'conv_b': jnp.zeros((3 * W,), jnp.float32), 'wq': jax.random.normal(ks[2], (W, H, dh), jnp.float32) * s(W), 'bq': jnp.zeros((H, dh), jnp.float32), 'wk': jax.random.normal(ks[3], (W, H, dh), jnp.float32) * s(W), 'bk': jnp.zeros((H, dh), jnp.float32), 'wv': jax.random.normal(ks[4], (W, H, dh), jnp.float32) * s(W), 'bv': jnp.zeros((H, dh), jnp.float32), 'wo': jax.random.normal(ks[5], (H, dh, W), jnp.float32) * s(H * dh), 'bo': jnp.zeros((W,), jnp.float32), 'proj_w': jax.random.normal(ks[6], (W, Dm), jnp.float32) * s(W), 'proj_b': jnp.zeros((Dm,), jnp.float32)}
    _L0_attn_in = _L0_attn_setup()

    def _L0_ffn_setup():
        import jax, jax.numpy as jnp
        import numpy as np
        SCALING = 16.0 / 8.0
        GAMMA = 1.0
        EPS = 1e-12
        key = jax.random.key(seed)
        ks = jax.random.split(key, 8)
        B, T, H, O = (4, 512, 1024, 1024)
        E_tot, E_act, r = (16, 4, 8)
        return {'x': jax.random.normal(ks[0], (B, T, H), jnp.float32), 'W_base': jax.random.normal(ks[1], (O, H), jnp.float32) * 0.02, 'b_base': jax.random.normal(ks[2], (O,), jnp.float32) * 0.02, 'lora_A': jax.random.normal(ks[3], (E_tot, r, H), jnp.float32) * 0.02, 'lora_B': jax.random.normal(ks[4], (E_tot, O, r), jnp.float32) * 0.02, 'router_W': jax.random.normal(ks[5], (E_tot, H), jnp.float32) * 0.02, 'router_b': jax.random.normal(ks[6], (E_tot,), jnp.float32) * 0.02, 'domain_prior': jax.random.uniform(ks[7], (E_tot,), jnp.float32), 'active': jnp.arange(E_act, dtype=jnp.int32)}
    _L0_ffn_in = _L0_ffn_setup()
    _d = {'L0_attn_inputs': _L0_attn_in['inputs'], 'L0_attn_conv_w': _L0_attn_in['conv_w'], 'L0_attn_conv_b': _L0_attn_in['conv_b'], 'L0_attn_wq': _L0_attn_in['wq'], 'L0_attn_bq': _L0_attn_in['bq'], 'L0_attn_wk': _L0_attn_in['wk'], 'L0_attn_bk': _L0_attn_in['bk'], 'L0_attn_wv': _L0_attn_in['wv'], 'L0_attn_bv': _L0_attn_in['bv'], 'L0_attn_wo': _L0_attn_in['wo'], 'L0_attn_bo': _L0_attn_in['bo'], 'L0_attn_proj_w': _L0_attn_in['proj_w'], 'L0_attn_proj_b': _L0_attn_in['proj_b'], 'L0_ffn_W_base': _L0_ffn_in['W_base'], 'L0_ffn_b_base': _L0_ffn_in['b_base'], 'L0_ffn_lora_A': _L0_ffn_in['lora_A'], 'L0_ffn_lora_B': _L0_ffn_in['lora_B'], 'L0_ffn_router_W': _L0_ffn_in['router_W'], 'L0_ffn_router_b': _L0_ffn_in['router_b'], 'L0_ffn_domain_prior': _L0_ffn_in['domain_prior'], 'L0_ffn_active': _L0_ffn_in['active']}
    _x0 = _d['L0_attn_inputs']
    _d['L0_attn_inputs'] = jax.random.normal(jax.random.fold_in(jax.random.key(seed), 1), (2, 1024, 1024), dtype=_x0.dtype)
    del _x0
    return _d

def reference(L0_attn_inputs, L0_attn_conv_w, L0_attn_conv_b, L0_attn_wq, L0_attn_bq, L0_attn_wk, L0_attn_bk, L0_attn_wv, L0_attn_bv, L0_attn_wo, L0_attn_bo, L0_attn_proj_w, L0_attn_proj_b, L0_ffn_W_base, L0_ffn_b_base, L0_ffn_lora_A, L0_ffn_lora_B, L0_ffn_router_W, L0_ffn_router_b, L0_ffn_domain_prior, L0_ffn_active):

    def _L0_attn_ref(inputs, conv_w, conv_b, wq, bq, wk, bk, wv, bv, wo, bo, proj_w, proj_b):
        import jax, jax.numpy as jnp
        import numpy as np
        from jax import lax
        BLOCK_LEN = 128
        NEG_INF = -1000000000.0
        N, L, Dm = inputs.shape
        x = lax.conv_general_dilated(inputs, conv_w, window_strides=(1,), padding='SAME', dimension_numbers=('NWC', 'WIO', 'NWC')) + conv_b
        q, k, v = jnp.split(x, 3, axis=-1)
        W_ = q.shape[-1]
        nb = L // BLOCK_LEN
        q = q.reshape(N * nb, BLOCK_LEN, W_)
        k = k.reshape(N * nb, BLOCK_LEN, W_)
        v = v.reshape(N * nb, BLOCK_LEN, W_)
        dh = wq.shape[-1]
        qh = jnp.einsum('btd,dhe->bthe', q, wq) + bq
        kh = jnp.einsum('btd,dhe->bthe', k, wk) + bk
        vh = jnp.einsum('btd,dhe->bthe', v, wv) + bv
        scale = 1.0 / jnp.sqrt(jnp.asarray(dh, qh.dtype))
        scores = jnp.einsum('bqhe,bkhe->bhqk', qh * scale, kh)
        causal = jnp.tril(jnp.ones((BLOCK_LEN, BLOCK_LEN), bool))
        scores = jnp.where(causal, scores, NEG_INF)
        p = jax.nn.softmax(scores, axis=-1)
        o = jnp.einsum('bhqk,bkhe->bqhe', p, vh)
        o = jnp.einsum('bqhe,hed->bqd', o, wo) + bo
        o = o.reshape(N, L, W_)
        return o @ proj_w + proj_b

    def _L0_ffn_ref(x, W_base, b_base, lora_A, lora_B, router_W, router_b, domain_prior, active):
        import jax, jax.numpy as jnp
        import numpy as np
        SCALING = 16.0 / 8.0
        GAMMA = 1.0
        EPS = 1e-12
        y = jnp.einsum('bth,oh->bto', x, W_base) + b_base
        A = lora_A[active]
        Bm = lora_B[active]
        z = jnp.einsum('bth,erh->bter', x, A)
        contribs = jnp.einsum('bter,eor->bteo', z, Bm) * SCALING
        logits = jnp.einsum('bth,eh->bte', x, router_W) + router_b
        logits = logits[..., active]
        prior = domain_prior[active]
        alpha = jax.nn.softmax(jnp.log(prior + EPS) + logits / GAMMA, axis=-1)
        return y + jnp.einsum('bteo,bte->bto', contribs, alpha)
    x = L0_attn_inputs
    x = x + _L0_attn_ref(_layernorm(x, axis=-1), L0_attn_conv_w, L0_attn_conv_b, L0_attn_wq, L0_attn_bq, L0_attn_wk, L0_attn_bk, L0_attn_wv, L0_attn_bv, L0_attn_wo, L0_attn_bo, L0_attn_proj_w, L0_attn_proj_b)
    x = x + _L0_ffn_ref(_layernorm(x, axis=-1), L0_ffn_W_base, L0_ffn_b_base, L0_ffn_lora_A, L0_ffn_lora_B, L0_ffn_router_W, L0_ffn_router_b, L0_ffn_domain_prior, L0_ffn_active)
    return x

_drawn_inputs = setup_inputs


def setup_inputs(seed=0):
    import zlib

    import numpy as np

    out = dict(_drawn_inputs(seed))
    spreads = {'L0_attn_conv_b': (0.0, 0.1),
     'L0_attn_bq': (0.0, 0.424),
     'L0_attn_bk': (0.0, 2.0),
     'L0_attn_bv': (0.0, 0.1),
     'L0_attn_bo': (0.0, 0.1),
     'L0_attn_proj_b': (0.0, 0.1)}
    factors = {'L0_ffn_b_base': 3.648,
     'L0_ffn_router_W': 3.846,
     'L0_ffn_router_b': 200.0,
     'L0_ffn_domain_prior': 200.0}
    for name, (base, spread) in spreads.items():
        noise = np.random.default_rng([zlib.crc32(name.encode()), seed]).standard_normal(out[name].shape)
        drawn = base * np.exp(spread * noise) if base else spread * noise
        out[name] = jnp.asarray(drawn.astype(out[name].dtype))
    for name, factor in factors.items():
        out[name] = (out[name] * factor).astype(out[name].dtype)
    return out
```

```python
from contextlib import ExitStack

import concourse.bass as bass
from concourse import mybir

F32 = mybir.dt.float32
F32R = mybir.dt.float32r
I32 = mybir.dt.int32
ALU = mybir.AluOpType
ACT = mybir.ActivationFunctionType
AX_X = mybir.AxisListType.X

P = 128
N, L, DM = 2, 1024, 1024
W, H, DH = 256, 16, 64
TOK = N * L
DC = DM // P
MC = 3 * W // P
WC = W // P
LT = L // P
PAIRS = L // 2
NV = 4
EPS = 1e-5
HW_ = H * DH
BANK = 512

E_TOT, E_ACT, RANK = 16, 4, 8
ER = E_ACT * RANK
PRIOR_EPS = 1e-12
LORA_SCALE = 16.0 / 8.0
MASKED = -1e30


def wait(eng, sem, count):
    if isinstance(count, int) and count <= 0:
        return
    eng.wait_ge(sem, count)


class Space:

    def __init__(self, nc, ctx, prefix):
        self.nc, self.ctx, self.prefix = nc, ctx, prefix

    def sb(self, name, shape, dtype=F32):
        return self.ctx.enter_context(self.nc.sbuf_tensor(f"{self.prefix}_{name}", shape, dtype))

    def ps(self, name, shape):
        return self.ctx.enter_context(self.nc.psum_tensor(f"{self.prefix}_{name}", shape, F32))

    def sem(self, name):
        return self.ctx.enter_context(self.nc.semaphore(f"{self.prefix}_{name}"))


def three_pass(pe, out, w_hi, w_lo, x_hi, x_lo, first, last):
    pe.matmul(out, w_hi, x_hi, start=first, stop=False)
    pe.matmul(out, w_hi, x_lo, start=False, stop=False)
    return pe.matmul(out, w_lo, x_hi, start=False, stop=last)


def conv_phase(nc, x, conv_w, c_dram, ident):
    with ExitStack() as ctx:
        sp = Space(nc, ctx, "conv")
        xn = sp.sb("xn", [P, LT, DM])
        xT = sp.sb("xT", [P, 2, L + 2])
        u = sp.sb("u", [P, 2, PAIRS])
        x_hi = sp.sb("x_hi", [P, DC, NV, PAIRS], F32R)
        x_lo = sp.sb("x_lo", [P, DC, NV, PAIRS], F32R)
        WR, RR = 4, 4
        raw = sp.sb("raw", [P, RR, 3, P])
        wsum = sp.sb("wsum", [P, 2, P])
        wmix = sp.sb("wmix", [P, 2, 2, P])
        w_hi = sp.sb("w_hi", [P, WR, NV, P], F32R)
        w_lo = sp.sb("w_lo", [P, WR, NV, P], F32R)
        p1 = sp.sb("p1", [P, PAIRS])
        y = sp.sb("y", [P, PAIRS, 2])
        stats = sp.sb("stats", [P, 2, 6])
        mv = sp.sb("mv", [P, LT, 2])
        vareps = sp.sb("vareps", [P, LT])
        rstd = sp.sb("rstd", [P, LT])
        mhalf = sp.sb("mhalf", [P, 1])

        acc = [sp.ps("acc_even", [P, NV, BANK]), sp.ps("acc_odd", [P, NV, BANK])]
        Q0, Q3, Q1, Q2 = 0, 1, 2, 3

        x_loaded = [sp.sem(f"x_loaded{j}") for j in range(LT)]
        raw_loaded = [sp.sem(f"raw_loaded{i}") for i in range(RR)]
        names = ("power_ready", "pads_ready", "stats_done", "mv_done", "var_ready", "rstd_ready", "xn_ready", "transposed", "xT_ready", "u_ready",
                 "x_hi_ready", "x_lo_ready", "wsum_ready", "wmix_ready", "w_hi_ready", "w_lo_ready", "unit_done",
                 "p1_ready", "mixed", "y_ready", "y_stored")
        s = {n: sp.sem(n) for n in names}
        block = ctx.enter_context(nc.Block())

        EVAC_AT = WR

        def before(n, m, st, store):
            if not isinstance(m, int):
                store(n, m - 1, st - 1)
            elif m:
                store(n, m - 1, st - 1)
            elif n:
                store(n - 1, MC - 1, st - 1)

        def steps(eng, n, one_step):
            for m in range(2):
                one_step(n, m, m % 2, MC * n + m)
            with eng.Fori(1, MC // 2) as k:
                for par in range(2):
                    one_step(n, 2 * k + par, par, 2 * k + (MC * n + par))

        @block.sync
        def _(sync):
            def load_step(n, m, par, st):
                for c in range(DC):
                    unit = DC * st + c
                    wait(sync, s["w_lo_ready"], unit - RR + 1)
                    sync.dma_start(raw[:, c % RR], conv_w[bass.ds(m, 1), :, c].rearrange("m p t o -> p (m t) o")).then_inc(raw_loaded[c % RR], 16)

            for n in range(N):
                wait(sync, s["transposed"], DC * n)
                for j in range(LT):
                    sync.dma_start(xn[:, j], x[n, j * P:(j + 1) * P, :]).then_inc(x_loaded[j], 16)
                steps(sync, n, load_step)

        @block.gpsimd
        def _(pool):
            pool.memset(mhalf[:], -0.5).then_inc(s["power_ready"], 1)

            def store(n, m, st):
                pool.wait_ge(s["y_ready"], st + 1)
                pool.dma_start(c_dram[n, bass.ds(m, 1)].rearrange("m p l -> p (m l)"), y[:].rearrange("p i k -> p (i k)")).then_inc(s["y_stored"], 16)

            def step(n, m, par, st):
                for c in range(DC):
                    unit = DC * st + c
                    if c == EVAC_AT:
                        before(n, m, st, store)
                    wait(pool, raw_loaded[c % RR], 16 * (DC // RR * st + c // RR + 1))
                    wait(pool, s["wmix_ready"], unit - 1)
                    pool.tensor_tensor(wsum[:, c % 2], raw[:, c % RR, 0], raw[:, c % RR, 2], ALU.add).then_inc(s["wsum_ready"], 1)
                    pool.wait_ge(s["wsum_ready"], unit + 1)
                    wait(pool, s["w_lo_ready"], unit - 1)
                    pool.tensor_tensor(wmix[:, c % 2, 0], wsum[:, c % 2], raw[:, c % RR, 1], ALU.add)
                    pool.tensor_tensor(wmix[:, c % 2, 1], wsum[:, c % 2], raw[:, c % RR, 1], ALU.subtract).then_inc(s["wmix_ready"], 1)
            for n in range(N):
                for j in range(LT):
                    pool.wait_ge(s["var_ready"], LT * n + j + 1)
                    if n == 0 and j == 0:
                        pool.wait_ge(s["power_ready"], 1)
                    pool.tensor_tensor(rstd[:, j:j + 1], vareps[:, j:j + 1], mhalf[:], ALU.pow).then_inc(s["rstd_ready"], 1)
                steps(pool, n, step)
            store(N - 1, MC - 1, MC * N - 1)
            pool.wait_ge(s["y_stored"], 16 * MC * N)

        @block.scalar
        def _(act):
            def chunk_in(n, c):
                k = DC * n + c
                act.wait_ge(s["transposed"], k + 1)
                wait(act, s["u_ready"], NV * (k - 1))
                act.activation(xT[:, c % 2, 1:L + 1], acc[1][:, 2 * (c % 2):2 * (c % 2) + 2, :], ACT.Copy).then_inc(s["xT_ready"], 1)
                for v in range(NV):
                    act.wait_ge(s["u_ready"], NV * k + v + 1)
                    if n:
                        act.wait_ge(s["unit_done"], DC * (MC * n - 1) + c + 1)
                    act.activation(x_hi[:, c, v], u[:, v % 2], ACT.Copy).then_inc(s["x_hi_ready"], 1)

            def evacuate(st, par):
                act.wait_ge(s["unit_done"], DC * st + DC)
                wait(act, s["mixed"], st)
                act.activation(p1[:], acc[par][:, Q1, :], ACT.Copy).then_inc(s["p1_ready"], 1)

            def step(n, m, par, st):
                first = isinstance(m, int) and m == 0
                for c in range(DC):
                    unit = DC * st + c
                    if c == (0 if first else EVAC_AT) and not (first and n == 0):
                        evacuate(st - 1, 1 - par)
                    if first:
                        chunk_in(n, c)
                    wait(act, s["unit_done"], unit - WR + 1)
                    act.wait_ge(raw_loaded[c % RR], 16 * (DC // RR * st + c // RR + 1))
                    act.activation(w_hi[:, c % WR, 0:2], raw[:, c % RR, 0:3:2], ACT.Copy)
                    act.wait_ge(s["wmix_ready"], unit + 1)
                    act.activation(w_hi[:, c % WR, 2:4], wmix[:, c % 2], ACT.Copy, scale=0.5).then_inc(s["w_hi_ready"], 1)

            for n in range(N):
                steps(act, n, step)
            evacuate(MC * N - 1, 1)

        @block.vector
        def _(dve):
            dve.memset(xT[:, :, 0:1], 0.0).then_inc(s["pads_ready"], 1)
            dve.memset(xT[:, :, L + 1:L + 2], 0.0).then_inc(s["pads_ready"], 1)

            def normalise(n):
                for j in range(LT):
                    k = LT * n + j
                    dve.wait_ge(x_loaded[j], 16 * (n + 1))
                    wait(dve, s["mv_done"], k)
                    dve.bn_stats(stats[:, 0], xn[:, j, 0:DM // 2])
                    dve.bn_stats(stats[:, 1], xn[:, j, DM // 2:DM]).then_inc(s["stats_done"], 1)
                    dve.wait_ge(s["stats_done"], k + 1)
                    dve.bn_aggr(mv[:, j], stats[:]).then_inc(s["mv_done"], 1)
                    dve.wait_ge(s["mv_done"], k + 1)
                    dve.tensor_scalar(vareps[:, j:j + 1], mv[:, j, 1:2], EPS, None, ALU.add).then_inc(s["var_ready"], 1)
                    if j:
                        scale(n, j - 1)
                scale(n, LT - 1)

            def scale(n, j):
                dve.wait_ge(s["rstd_ready"], LT * n + j + 1)
                dve.tensor_scalar(xn[:, j], xn[:, j], mv[:, j, 0:1], rstd[:, j:j + 1], ALU.subtract, ALU.mult).then_inc(s["xn_ready"], 1)

            def split_input(n, c, v):
                k = DC * n + c
                d = [xT[:, c % 2, a:a + 2 * PAIRS - 1:2] for a in range(4)]
                a, b, op = ((d[0], d[2], ALU.subtract), (d[3], d[1], ALU.subtract), (d[1], d[2], ALU.add), (d[2], d[1], ALU.subtract))[v]
                dve.tensor_tensor(u[:, v % 2], a, b, op).then_inc(s["u_ready"], 1)

            def low_input(n, c, v):
                dve.wait_ge(s["x_hi_ready"], NV * (DC * n + c) + v + 1)
                dve.tensor_tensor(x_lo[:, c, v], u[:, v % 2], x_hi[:, c, v], ALU.subtract).then_inc(s["x_lo_ready"], 1)

            def chunk_in(n, c):
                k = DC * n + c
                if k == 0:
                    dve.wait_ge(s["pads_ready"], 2)
                dve.wait_ge(s["xT_ready"], k + 1)
                for v in range(NV):
                    if v >= 2:
                        dve.wait_ge(s["x_lo_ready"], NV * k + v - 1)
                    elif k:
                        dve.wait_ge(s["x_lo_ready"], NV * (k - 1) + v + 3)
                    split_input(n, c, v)
                    if v:
                        low_input(n, c, v - 1)
                low_input(n, c, NV - 1)

            def outputs(st, par):
                dve.wait_ge(s["p1_ready"], st + 1)
                wait(dve, s["y_stored"], 16 * st)
                dve.tensor_tensor(y[:, :, 0], acc[par][:, Q2, :], p1[:], ALU.add)
                dve.tensor_tensor(y[:, :, 1], p1[:], acc[par][:, Q2, :], ALU.subtract).then_inc(s["mixed"], 1)
                dve.wait_ge(s["mixed"], st + 1)
                dve.tensor_tensor(y[:, :, 0], acc[par][:, Q0, :], y[:, :, 0], ALU.add)
                dve.tensor_tensor(y[:, :, 1], acc[par][:, Q3, :], y[:, :, 1], ALU.add).then_inc(s["y_ready"], 1)

            def step(n, m, par, st):
                first = isinstance(m, int) and m == 0
                for c in range(DC):
                    unit = DC * st + c
                    if c == (0 if first else EVAC_AT) and not (first and n == 0):
                        outputs(st - 1, 1 - par)
                    if first:
                        chunk_in(n, c)
                    dve.wait_ge(s["w_hi_ready"], unit + 1)
                    dve.tensor_tensor(w_lo[:, c % WR, 0:2], raw[:, c % RR, 0:3:2], w_hi[:, c % WR, 0:2], ALU.subtract)
                    dve.scalar_tensor_tensor(w_lo[:, c % WR, 2:4], wmix[:, c % 2], 0.5, w_hi[:, c % WR, 2:4], ALU.mult, ALU.subtract).then_inc(s["w_lo_ready"], 1)

            for n in range(N):
                normalise(n)
                steps(dve, n, step)
            outputs(MC * N - 1, 1)

        @block.tensor
        def _(pe):
            def transpose_chunk(n, c):
                k = DC * n + c
                if c == 0:
                    wait(pe, s["y_ready"], MC * n)
                if c >= 2:
                    pe.wait_ge(s["xT_ready"], k - 1)
                for j in range(LT):
                    if c == 0:
                        pe.wait_ge(s["xn_ready"], LT * n + j + 1)
                    o = acc[1][:, 2 * (c % 2) + j // 4, (j % 4) * P:(j % 4 + 1) * P]
                    t = pe.transpose(o, xn[:, j, c * P:(c + 1) * P], ident[:])
                t.then_inc(s["transposed"], 1)

            def step(n, m, par, st):
                if isinstance(m, int) and m == 0:
                    transpose_chunk(n, 0)
                if isinstance(m, int) and m == 1:
                    pe.wait_ge(s["xT_ready"], DC * (n + 1))
                else:
                    wait(pe, s["y_ready"], st - 1)
                for c in range(DC):
                    unit = DC * st + c
                    if isinstance(m, int) and m == 0:
                        if c + 1 < DC:
                            transpose_chunk(n, c + 1)
                        pe.wait_ge(s["x_lo_ready"], NV * (DC * n + c + 1))
                    pe.wait_ge(s["w_lo_ready"], unit + 1)
                    for v in range(NV):
                        mm = three_pass(pe, acc[par][:, v, :], w_hi[:, c % WR, v], w_lo[:, c % WR, v],
                                        x_hi[:, c, v], x_lo[:, c, v], c == 0, c == DC - 1)
                    mm.then_inc(s["unit_done"], 1)

            for n in range(N):
                steps(pe, n, step)


def attention_phase(nc, x, c_dram, conv_b, wq, wk, wv, wo, pw, bq, bk, bv, bo, pb, x1, ident):
    GB = 2
    GT = GB * P
    NG = TOK // GT
    GL = L // GT
    NP = H // 2
    UN = 2 * GB
    OC = HW_ // P
    QKW = 2 * GT
    with ExitStack() as ctx:
        sp = Space(nc, ctx, "attn")
        stage = sp.sb("stage", [P, 2, 1024])
        wqkv_hi = sp.sb("wqkv_hi", [P, 3, WC, HW_], F32R)
        wqkv_lo = sp.sb("wqkv_lo", [P, 3, WC, HW_], F32R)
        wo_hi = sp.sb("wo_hi", [P, OC, W], F32R)
        wo_lo = sp.sb("wo_lo", [P, OC, W], F32R)
        pw_hi = sp.sb("pw_hi", [P, WC, DM], F32R)
        pw_lo = sp.sb("pw_lo", [P, WC, DM], F32R)
        cb_c = sp.sb("cb_c", [P, MC])
        bqk_c = sp.sb("bqk_c", [P, 2, NP])
        bv_c = sp.sb("bv_c", [P, OC])
        bo_c = sp.sb("bo_c", [P, WC])
        ba_c = sp.sb("ba_c", [P, WC])
        pb_r = sp.sb("pb_r", [P, DM])
        mask = sp.sb("mask", [P, GB, P])
        c_raw = sp.sb("c_raw", [P, MC, GT])
        c_hi = sp.sb("c_hi", [P, MC, GT], F32R)
        c_lo = sp.sb("c_lo", [P, MC, GT], F32R)
        v_hi = sp.sb("v_hi", [P, GB, HW_], F32R)
        v_lo = sp.sb("v_lo", [P, GB, HW_], F32R)
        qk_hi = sp.sb("qk_hi", [P, 2, 2, GT], F32R)
        qk_lo = sp.sb("qk_lo", [P, 2, 2, GT], F32R)
        pr = sp.sb("pr", [P, 2, UN, P])
        negmax = sp.sb("negmax", [P, 2, UN])
        rsum = sp.sb("rsum", [P, 4, UN])
        rrec = sp.sb("rrec", [P, 4, UN])
        pT_hi = sp.sb("pT_hi", [P, 2, UN, P], F32R)
        pT_lo = sp.sb("pT_lo", [P, 2, UN, P], F32R)
        o_n = sp.sb("o_n", [P, GB, HW_])
        oT_hi = sp.sb("oT_hi", [P, OC, GT], F32R)
        oT_lo = sp.sb("oT_lo", [P, OC, GT], F32R)
        a_hi = sp.sb("a_hi", [P, WC, GT], F32R)
        a_lo = sp.sb("a_lo", [P, WC, GT], F32R)
        xr = sp.sb("xr", [P, GB, DM])

        scp = sp.ps("scp", [P, 2, BANK])
        qkp = sp.ps("qkp", [P, QKW])
        ptp = sp.ps("ptp", [P, UN, P])
        op = sp.ps("op", [P, BANK])
        gp = sp.ps("gp", [P, 3, BANK])

        names = ("bias_loaded", "x_loaded", "c_loaded", "w_hi_ready", "w_lo_ready", "bvo_done", "ba_part", "ba_ready", "mask0", "mask_ready",
                 "c_hi_ready", "c_lo_ready", "v_done", "v_hi_ready", "v_lo_ready", "qk_done", "qk_hi_ready", "qk_lo_ready",
                 "sc_done", "sm_ready", "max_ready", "exp_ready", "pT_done", "pT_hi_ready", "pT_lo_ready",
                 "rrec_ready", "o_done", "o_ready", "oT_done", "oT_hi_ready", "oT_lo_ready", "a_done", "a_hi_ready", "a_lo_ready",
                 "xb_ready", "y_done", "x1_ready", "x1_stored")
        s = {n: sp.sem(n) for n in names}
        w_loaded = [sp.sem(f"w_loaded{i}") for i in range(2)]
        block = ctx.enter_context(nc.Block())

        pieces = [(src[:, i], hi[:, i], lo[:, i]) for src, hi, lo in
                  [(w.rearrange("p c n -> p c n"), wqkv_hi[:, k], wqkv_lo[:, k]) for k, w in enumerate((wq, wk, wv))] for i in range(WC)]
        pieces += [(wo[:, 4 * i:4 * i + 4], wo_hi[:, 4 * i:4 * i + 4], wo_lo[:, 4 * i:4 * i + 4]) for i in range(2)]
        pieces += [(pw[:, i], pw_hi[:, i], pw_lo[:, i]) for i in range(WC)]
        NW = len(pieces)
        WO_AT = 6

        def slot(i, like):
            st = stage[:, i % 2]
            return st.rearrange("p (a b) -> p a b", a=4) if len(like.shape) == 3 else st

        VT = GB * HW_ // BANK
        OT = GB * OC // 4
        YT = GB * DM // BANK

        def groups(eng, one_group):
            one_group(0, 0, 0)
            with eng.Fori(1, GL) as r:
                one_group(r, 0, r)
            with eng.Fori(0, GL) as r:
                one_group(r + GL, 1, r)

        @block.sync
        def _(sync):
            def load(b, r):
                sync.dma_start(c_raw[:], c_dram[b, :, :, bass.ds(GT * r, GT)].rearrange("m p l -> p m l")).then_inc(s["c_loaded"], 16)

            for i in range(NW):
                if i == 2:
                    sync.dma_start(cb_c[:], conv_b).then_inc(s["bias_loaded"], 16)
                    load(0, 0)
                    for dst, src in ((bqk_c[:, 0], bq), (bqk_c[:, 1], bk), (bv_c[:], bv), (bo_c[:], bo)):
                        sync.dma_start(dst, src).then_inc(s["bias_loaded"], 16)
                    sync.dma_start(pb_r[:], pb.to_broadcast([P, DM])).then_inc(s["bias_loaded"], 16)
                wait(sync, s["w_lo_ready"], i - 1)
                if i >= WO_AT + 2:
                    sync.wait_ge(s["bvo_done"], i - WO_AT - 1)
                sync.dma_start(slot(i, pieces[i][0]), pieces[i][0]).then_inc(w_loaded[i % 2], 16)

            def x_rows(t, b, r):
                return t[b, bass.ds(GT * r, GT), :].rearrange("(k p) d -> p k d", p=P)

            def store(g, b, r):
                sync.wait_ge(s["x1_ready"], YT * (g + 1))
                sync.dma_start(x_rows(x1, b, r), xr[:]).then_inc(s["x1_stored"], 16)

            def group(g, b, r):
                if not (isinstance(g, int) and g == 0):
                    sync.wait_ge(s["c_lo_ready"], MC * g)
                    load(b, r)
                    sync.wait_ge(s["x1_stored"], 16 * g)
                sync.dma_start(xr[:], x_rows(x, b, r)).then_inc(s["x_loaded"], 16)
                store(g, b, r)

            groups(sync, group)
            sync.wait_ge(s["x1_stored"], 16 * NG)

        @block.gpsimd
        def _(pool):
            pool.memset(mask[:], 0.0).then_inc(s["mask0"], 1)
            pool.wait_ge(s["mask0"], 1)
            pool.affine_select(out=mask[:], in_=mask[:], compare_op=ALU.is_ge, fill=MASKED, base=0,
                               pattern=[[0, GB], [-1, P]], channel_multiplier=1).then_inc(s["mask_ready"], 1)
            pool.wait_ge(s["bias_loaded"], 16 * 6)

            def group(g, b, r):
                pool.wait_ge(s["x_loaded"], 16 * (g + 1))
                for k in range(GB):
                    pool.tensor_tensor(xr[:, k], xr[:, k], pb_r[:], ALU.add).then_inc(s["xb_ready"], 1)

            groups(pool, group)

        STEPS = NP + 3

        @block.scalar
        def _(act):
            for i in range(NW):
                src, hi, lo = pieces[i]
                act.wait_ge(w_loaded[i % 2], 16 * (i // 2 + 1))
                act.activation(hi, slot(i, src), ACT.Copy).then_inc(s["w_hi_ready"], 1)
            act.wait_ge(s["bias_loaded"], 16 * 6)

            def group(g, b, r):
                act.wait_ge(s["c_loaded"], 16 * (g + 1))
                for m in (4, 5, 0, 2, 1, 3):
                    if m == 4:
                        wait(act, s["v_done"], VT * g)
                        wait(act, s["qk_done"], NP * g)
                    act.activation(c_hi[:, m], c_raw[:, m], ACT.Identity, bias=cb_c[:, m:m + 1]).then_inc(s["c_hi_ready"], 1)
                for i in range(VT):
                    act.wait_ge(s["v_done"], VT * g + i + 1)
                    if i == 0:
                        wait(act, s["o_done"], NP * g)
                    act.activation(v_hi[:, i // 2, (i % 2) * BANK:(i % 2 + 1) * BANK], gp[:, i % 3], ACT.Copy).then_inc(s["v_hi_ready"], 1)
                for i in range(STEPS):
                    if i < NP:
                        j = i
                        act.wait_ge(s["qk_done"], NP * g + j + 1)
                        wait(act, s["sc_done"], NP * g + j - 1)
                        for k in range(2):
                            act.activation(qk_hi[:, j % 2, k], qkp[:, k * GT:(k + 1) * GT], ACT.Identity,
                                           bias=bqk_c[:, k, j:j + 1]).then_inc(s["qk_hi_ready"], 1)
                    if 1 <= i <= NP:
                        j = i - 1
                        act.wait_ge(s["max_ready"], NP * g + j + 1)
                        wait(act, s["rrec_ready"], NP * g + j - 3)
                        for un in range(UN):
                            act.activation(pr[:, j % 2, un], pr[:, j % 2, un], ACT.Exp, bias=negmax[:, j % 2, un:un + 1],
                                           accum_out=rsum[:, j % 4, un:un + 1]).then_inc(s["exp_ready"], 1)
                    if 2 <= i <= NP + 1:
                        j = i - 2
                        act.wait_ge(s["pT_done"], NP * g + j + 1)
                        wait(act, s["o_done"], NP * g + j - 1)
                        act.activation(pT_hi[:, j % 2], ptp[:], ACT.Copy).then_inc(s["pT_hi_ready"], 1)
                for i in range(OT):
                    act.wait_ge(s["oT_done"], OT * g + i + 1)
                    if i == 0:
                        wait(act, s["a_done"], g)
                    act.activation(oT_hi[:, 4 * (i % 2):4 * (i % 2) + 4, (i // 2) * P:(i // 2 + 1) * P],
                                   gp[:, i % 3].rearrange("p (c t) -> p c t", c=4), ACT.Copy).then_inc(s["oT_hi_ready"], 1)
                act.wait_ge(s["a_done"], g + 1)
                act.wait_ge(s["ba_ready"], 1)
                wait(act, s["y_done"], YT * g)
                for d in range(WC):
                    act.activation(a_hi[:, d], gp[:, OT % 3, d * GT:(d + 1) * GT], ACT.Identity, bias=ba_c[:, d:d + 1]).then_inc(s["a_hi_ready"], 1)

            groups(act, group)

        @block.vector
        def _(dve):
            def weight(i):
                src, hi, lo = pieces[i]
                dve.wait_ge(s["w_hi_ready"], i + 1)
                dve.tensor_tensor(lo, slot(i, src), hi, ALU.subtract).then_inc(s["w_lo_ready"], 1)

            for i in range(NW):
                weight(i)
            dve.wait_ge(s["bias_loaded"], 16 * 6)
            dve.wait_ge(s["bvo_done"], 2)
            dve.tensor_tensor(ba_c[:], op[:, 0:WC], bo_c[:], ALU.add).then_inc(s["ba_part"], 1)
            dve.wait_ge(s["ba_part"], 1)
            dve.tensor_tensor(ba_c[:], ba_c[:], op[:, WC:2 * WC], ALU.add).then_inc(s["ba_ready"], 1)

            def low(out, src, bias, hi):
                return dve.scalar_tensor_tensor(out, src, bias, hi, ALU.add, ALU.subtract)

            def group(g, b, r):
                for n, m in enumerate((4, 5, 0, 2, 1, 3)):
                    dve.wait_ge(s["c_hi_ready"], MC * g + n + 1)
                    low(c_lo[:, m], c_raw[:, m], cb_c[:, m:m + 1], c_hi[:, m]).then_inc(s["c_lo_ready"], 1)
                for i in range(VT):
                    dve.wait_ge(s["v_hi_ready"], VT * g + i + 1)
                    cols = slice((i % 2) * BANK, (i % 2 + 1) * BANK)
                    dve.tensor_tensor(v_lo[:, i // 2, cols], gp[:, i % 3], v_hi[:, i // 2, cols], ALU.subtract).then_inc(s["v_lo_ready"], 1)
                for i in range(STEPS):
                    if i < NP:
                        j = i
                        dve.wait_ge(s["qk_hi_ready"], 2 * (NP * g + j) + 2)
                        for k in range(2):
                            low(qk_lo[:, j % 2, k], qkp[:, k * GT:(k + 1) * GT], bqk_c[:, k, j:j + 1], qk_hi[:, j % 2, k]).then_inc(s["qk_lo_ready"], 1)
                    if 1 <= i <= NP:
                        j = i - 1
                        if isinstance(g, int) and g == 0 and j == 0:
                            dve.wait_ge(s["mask_ready"], 1)
                        dve.wait_ge(s["sc_done"], NP * g + j + 1)
                        wait(dve, s["pT_done"], NP * g + j - 1)
                        dve.scalar_tensor_tensor(pr[:, j % 2].rearrange("p (h b) k -> p h (b k)", h=2), scp[:, :, 0:GT], DH ** -0.5,
                                                 mask[:].rearrange("p b k -> p (b k)").unsqueeze(1).to_broadcast([P, 2, GT]),
                                                 ALU.mult, ALU.add).then_inc(s["sm_ready"], 1)
                        dve.wait_ge(s["sm_ready"], NP * g + j + 1)
                        dve.tensor_reduce(negmax[:, j % 2], pr[:, j % 2], AX_X, ALU.max, negate=True).then_inc(s["max_ready"], 1)
                    if 2 <= i <= NP + 1:
                        j = i - 2
                        dve.wait_ge(s["pT_hi_ready"], NP * g + j + 1)
                        dve.tensor_tensor(pT_lo[:, j % 2], ptp[:], pT_hi[:, j % 2], ALU.subtract).then_inc(s["pT_lo_ready"], 1)
                        dve.wait_ge(s["exp_ready"], UN * (NP * g + j + 1))
                        dve.reciprocal(rrec[:, j % 4], rsum[:, j % 4]).then_inc(s["rrec_ready"], 1)
                    if i >= 3:
                        j = i - 3
                        dve.wait_ge(s["rrec_ready"], NP * g + j + 1)
                        dve.wait_ge(s["o_done"], NP * g + j + 1)
                        if j == 0:
                            wait(dve, s["oT_done"], OT * g)
                        dve.tensor_tensor(o_n[:, :, 2 * j * DH:(2 * j + 2) * DH].rearrange("p b (h e) -> p h b e", h=2),
                                          op[:, 0:UN * DH].rearrange("p (h b e) -> p h b e", h=2, b=GB),
                                          rrec[:, j % 4].rearrange("p (h b) -> p h b", h=2).unsqueeze(3).to_broadcast([P, 2, GB, DH]),
                                          ALU.mult).then_inc(s["o_ready"], 1)
                for i in range(OT):
                    dve.wait_ge(s["oT_hi_ready"], OT * g + i + 1)
                    part = (slice(4 * (i % 2), 4 * (i % 2) + 4), slice((i // 2) * P, (i // 2 + 1) * P))
                    dve.tensor_tensor(oT_lo[:, part[0], part[1]], gp[:, i % 3].rearrange("p (c t) -> p c t", c=4),
                                      oT_hi[:, part[0], part[1]], ALU.subtract).then_inc(s["oT_lo_ready"], 1)
                dve.wait_ge(s["a_hi_ready"], WC * g + WC)
                for d in range(WC):
                    low(a_lo[:, d], gp[:, OT % 3, d * GT:(d + 1) * GT], ba_c[:, d:d + 1], a_hi[:, d]).then_inc(s["a_lo_ready"], 1)
                for i in range(YT):
                    dve.wait_ge(s["y_done"], YT * g + i + 1)
                    if i == 0:
                        dve.wait_ge(s["xb_ready"], GB * (g + 1))
                    cols = slice((i % 2) * BANK, (i % 2 + 1) * BANK)
                    dve.tensor_tensor(xr[:, i // 2, cols], gp[:, (OT + 1 + i) % 3], xr[:, i // 2, cols], ALU.add).then_inc(s["x1_ready"], 1)

            groups(dve, group)

        @block.tensor
        def _(pe):
            def setup_bias():
                pe.wait_ge(s["bias_loaded"], 16 * 6)
                for i in range(2):
                    pe.wait_ge(w_loaded[(WO_AT + i) % 2], 16 * ((WO_AT + i) // 2 + 1))
                    raw = slot(WO_AT + i, pieces[WO_AT][0])
                    for d in range(WC):
                        for c in range(4):
                            mm = pe.matmul(op[:, WC * i + d:WC * i + d + 1], raw[:, c, d * P:(d + 1) * P], bv_c[:, 4 * i + c:4 * i + c + 1],
                                           start=(c == 0), stop=(c == 3))
                    mm.then_inc(s["bvo_done"], 1)

            def group(g, b, r):
                first = isinstance(g, int) and g == 0
                pe.wait_ge(s["c_lo_ready"], MC * g + 2)
                if first:
                    pe.wait_ge(s["w_lo_ready"], 6)
                for i in range(VT):
                    if i < 3:
                        wait(pe, s["x1_ready"], YT * g)
                    else:
                        pe.wait_ge(s["v_lo_ready"], VT * g + i - 2)
                    k, h = i // 2, i % 2
                    for c in range(WC):
                        mm = three_pass(pe, gp[:, i % 3], c_hi[:, 4 + c, k * P:(k + 1) * P], c_lo[:, 4 + c, k * P:(k + 1) * P],
                                        wqkv_hi[:, 2, c, h * BANK:(h + 1) * BANK], wqkv_lo[:, 2, c, h * BANK:(h + 1) * BANK], c == 0, c == WC - 1)
                    mm.then_inc(s["v_done"], 1)
                pe.wait_ge(s["c_lo_ready"], MC * (g + 1))
                for i in range(STEPS):
                    if i < NP:
                        j = i
                        wait(pe, s["qk_lo_ready"], 2 * (NP * g + j))
                        for k in range(2):
                            for c in range(WC):
                                mm = three_pass(pe, qkp[:, k * GT:(k + 1) * GT], wqkv_hi[:, k, c, j * P:(j + 1) * P], wqkv_lo[:, k, c, j * P:(j + 1) * P],
                                                c_hi[:, 2 * k + c], c_lo[:, 2 * k + c], c == 0, c == WC - 1)
                        mm.then_inc(s["qk_done"], 1)
                    if 1 <= i <= NP:
                        j = i - 1
                        pe.wait_ge(s["qk_lo_ready"], 2 * (NP * g + j + 1))
                        wait(pe, s["sm_ready"], NP * g + j)
                        for k in range(GB):
                            t = slice(k * P, (k + 1) * P)
                            for n, (ql, kl) in enumerate(((qk_hi, qk_hi), (qk_hi, qk_lo), (qk_lo, qk_hi))):
                                for h in range(2):
                                    e = slice(h * DH, (h + 1) * DH)
                                    mm = pe.matmul(scp[:, h, t], ql[e, j % 2, 0, t], kl[e, j % 2, 1, t], start=(n == 0), stop=(n == 2))
                        mm.then_inc(s["sc_done"], 1)
                    if 2 <= i <= NP + 1:
                        j = i - 2
                        pe.wait_ge(s["exp_ready"], UN * (NP * g + j + 1))
                        wait(pe, s["pT_lo_ready"], NP * g + j)
                        for un in range(UN):
                            mm = pe.transpose(ptp[:, un], pr[:, j % 2, un], ident[:])
                        mm.then_inc(s["pT_done"], 1)
                    if i >= 3:
                        j = i - 3
                        pe.wait_ge(s["pT_lo_ready"], NP * g + j + 1)
                        wait(pe, s["o_ready"], NP * g + j)
                        if first and j == 0:
                            pe.wait_ge(s["ba_ready"], 1)
                        if j == 0:
                            pe.wait_ge(s["v_lo_ready"], VT * (g + 1))
                        for h in range(2):
                            for k in range(GB):
                                un = GB * h + k
                                v = slice((2 * j + h) * DH, (2 * j + h + 1) * DH)
                                mm = three_pass(pe, op[:, un * DH:(un + 1) * DH], pT_hi[:, j % 2, un], pT_lo[:, j % 2, un],
                                                v_hi[:, k, v], v_lo[:, k, v], True, True)
                        mm.then_inc(s["o_done"], 1)
                pe.wait_ge(s["o_ready"], NP * (g + 1))
                for i in range(OT):
                    if i == 3:
                        pe.wait_ge(s["oT_lo_ready"], OT * g + 1)
                    for c in range(4):
                        oc = 4 * (i % 2) + c
                        mm = pe.transpose(gp[:, i % 3, c * P:(c + 1) * P], o_n[:, i // 2, oc * P:(oc + 1) * P], ident[:])
                    mm.then_inc(s["oT_done"], 1)
                if first:
                    pe.wait_ge(s["w_lo_ready"], NW)
                pe.wait_ge(s["oT_lo_ready"], OT * (g + 1))
                for d in range(WC):
                    for c in range(OC):
                        mm = three_pass(pe, gp[:, OT % 3, d * GT:(d + 1) * GT], wo_hi[:, c, d * P:(d + 1) * P], wo_lo[:, c, d * P:(d + 1) * P],
                                        oT_hi[:, c], oT_lo[:, c], c == 0, c == OC - 1)
                mm.then_inc(s["a_done"], 1)
                pe.wait_ge(s["a_lo_ready"], WC * (g + 1))
                for i in range(YT):
                    if i == 3:
                        pe.wait_ge(s["x1_ready"], YT * g + 1)
                    k, h = i // 2, i % 2
                    for c in range(WC):
                        mm = three_pass(pe, gp[:, (OT + 1 + i) % 3], a_hi[:, c, k * P:(k + 1) * P], a_lo[:, c, k * P:(k + 1) * P],
                                        pw_hi[:, c, h * BANK:(h + 1) * BANK], pw_lo[:, c, h * BANK:(h + 1) * BANK], c == 0, c == WC - 1)
                    mm.then_inc(s["y_done"], 1)

            setup_bias()
            groups(pe, group)


def ffn_phase(nc, x1, w_base, b_base, lora_a, lora_b, router_w, router_b, prior, active, out, ident):
    TT = TOK // P
    NH = DM // BANK
    Z = ER + E_ACT
    with ExitStack() as ctx:
        sp = Space(nc, ctx, "ffn")
        w_raw = sp.sb("w_raw", [P, 2, 2, DM])
        w_hi = sp.sb("w_hi", [P, DC, DM], F32R)
        w_lo = sp.sb("w_lo", [P, DC, DM], F32R)
        a_raw = sp.sb("a_raw", [P, DC, ER])
        r_raw = sp.sb("r_raw", [P, E_ACT, DC])
        az_hi = sp.sb("az_hi", [P, DC, Z], F32R)
        az_lo = sp.sb("az_lo", [P, DC, Z], F32R)
        act_sb = sp.sb("active", [1, E_ACT], I32)
        b_raw = sp.sb("b_raw", [ER + 1, DM])
        b_hi = sp.sb("b_hi", [ER + 1, DM], F32R)
        b_lo = sp.sb("b_lo", [ER + 1, DM], F32R)
        KB = 3 * ER + 2
        b_stack = sp.sb("b_stack", [KB, DM], F32R)
        lbias = sp.sb("lbias", [P, 2, E_ACT])
        logp = sp.sb("logp", [P, E_ACT])
        lsum = sp.sb("lsum", [P, E_ACT])
        x1t = sp.sb("x1t", [P, 4, DM])
        xn = sp.sb("xn", [P, 2, DM])
        xT_hi = sp.sb("xT_hi", [P, 2, DC, P], F32R)
        xT_lo = sp.sb("xT_lo", [P, 2, DC, P], F32R)
        y = sp.sb("y", [P, 2, DM])
        stats = sp.sb("stats", [P, 2, 2, 6])
        mv = sp.sb("mv", [P, 2, 2])
        vareps = sp.sb("vareps", [P, 2, 1])
        rstd = sp.sb("rstd", [P, 2, 1])
        mhalf = sp.sb("mhalf", [P, 1])
        logit = sp.sb("logit", [P, E_ACT])
        negmax = sp.sb("negmax", [P, 1])
        expl = sp.sb("expl", [P, E_ACT])
        esum = sp.sb("esum", [P, 1])
        erec = sp.sb("erec", [P, 1])
        alpha = sp.sb("alpha", [P, E_ACT])
        az = sp.sb("az", [P, ER])
        azs = sp.sb("azs", [P, 2, KB], F32R)
        azsT = sp.sb("azsT", [KB, 2, P], F32R)

        tp = sp.ps("tp", [P, 2, BANK])
        zp = sp.ps("zp", [P, BANK])
        ap = sp.ps("ap", [P, BANK])
        yp = sp.ps("yp", [P, 2, NH, BANK])

        names = ("active_loaded", "az_loaded", "b_loaded", "lbias_loaded", "az_split_hi", "az_split_lo", "b_split_hi", "b_split_lo", "b_stacked",
                 "w_hi_ready", "w_lo_ready", "logp_in", "logp_ready", "lsum_ready", "ones_ready", "power_ready",
                 "stats_done", "mv_done", "var_ready", "rstd_ready", "xn_ready", "transposed", "xT_hi_ready", "xT_lo_ready",
                 "z_done", "logit_ready", "max_ready", "exp_ready", "rec_ready", "alpha_ready", "az_ready", "azs_hi_ready", "azs_ready",
                 "azT_done", "azsT_ready", "y_done", "y_ready")
        s = {n: sp.sem(n) for n in names}
        w_loaded = [sp.sem(f"w_loaded{i}") for i in range(2)]
        x_loaded = [sp.sem(f"x_loaded{i}") for i in range(4)]
        y_stored = [sp.sem(f"y_stored{i}") for i in range(2)]
        block = ctx.enter_context(nc.Block())

        def tiles(eng, one_tile, lo=0):
            for q in range(4):
                one_tile(q, q)
            with eng.Fori(1, TT // 4 - 1) as k:
                for q in range(4):
                    one_tile(4 * k + q, q)
            for q in range(4):
                one_tile(TT - 4 + q, q)

        def is_last(t):
            return isinstance(t, int) and t == TT - 1

        @block.sync
        def _(sync):
            sync.dma_start(act_sb[:], active).then_inc(s["active_loaded"], 16)

            def load(t, q):
                wait(sync, s["y_ready"], NH * (t - 3))
                sync.dma_start(x1t[:, q], x1[bass.ds(t * P, P)]).then_inc(x_loaded[q], 16)

            load(0, 0)
            for i in range(DC // 2):
                wait(sync, s["w_lo_ready"], i - 1)
                sync.dma_start(w_raw[:, i % 2], w_base[:, 2 * i:2 * i + 2]).then_inc(w_loaded[i % 2], 16)
                if i == 0:
                    sync.wait_ge(s["active_loaded"], 16)
                    for e in range(E_ACT):
                        expert = sync.value_load(act_sb[0:1, e:e + 1], min_val=0, max_val=E_TOT - 1)
                        sync.dma_start(a_raw[:, :, e * RANK:(e + 1) * RANK], lora_a[bass.ds(expert, 1)].rearrange("e p c r -> (e p) c r")).then_inc(s["az_loaded"], 16)
                        sync.dma_start(r_raw[:, e], router_w[bass.ds(expert, 1)].rearrange("e p c -> (e p) c")).then_inc(s["az_loaded"], 16)
                        sync.dma_start(b_raw[e * RANK:(e + 1) * RANK, :], lora_b[bass.ds(expert, 1)].rearrange("e r o -> (e r) o")).then_inc(s["b_loaded"], 16)
                        sync.dma_start(lbias[:, 0, e:e + 1], router_b[bass.ds(expert, 1), :].to_broadcast([P, 1])).then_inc(s["lbias_loaded"], 16)
                        sync.dma_start(lbias[:, 1, e:e + 1], prior[bass.ds(expert, 1), :].to_broadcast([P, 1])).then_inc(s["lbias_loaded"], 16)
                    sync.dma_start(b_raw[ER:ER + 1, :], b_base).then_inc(s["b_loaded"], 16)
                if i == 1:
                    for t in range(1, 4):
                        load(t, t)
            sync.wait_ge(s["b_split_lo"], 1)
            for n, (part, r0, r1, at) in enumerate(((b_hi, 0, ER, 0), (b_hi, 0, ER, ER), (b_lo, 0, ER, 2 * ER),
                                                    (b_hi, ER, ER + 1, 3 * ER), (b_lo, ER, ER + 1, 3 * ER + 1))):
                sync.dma_start(b_stack[at:at + r1 - r0, :].bitcast(F32), part[r0:r1, :].bitcast(F32)).then_inc(s["b_stacked"], 16)

            def later(t, q):
                if not (isinstance(t, int) and t < 4):
                    load(t, q)

            tiles(sync, later)

        @block.gpsimd
        def _(pool):
            pool.memset(mhalf[:], -0.5).then_inc(s["power_ready"], 1)
            pool.wait_ge(s["power_ready"], 1)

            def power(t, q):
                pool.wait_ge(s["var_ready"], t + 1)
                pool.tensor_tensor(rstd[:, q % 2], vareps[:, q % 2], mhalf[:], ALU.pow).then_inc(s["rstd_ready"], 1)

            def store(t, q):
                pool.wait_ge(s["y_ready"], NH * (t + 1))
                pool.dma_start(out[bass.ds(t * P, P)], y[:, q % 2]).then_inc(y_stored[q % 2], 16)

            def tile(t, q):
                if isinstance(t, int) and t == 0:
                    power(0, 0)
                if not is_last(t):
                    power(t + 1, (q + 1) % 4)
                store(t, q)

            tiles(pool, tile)
            for par in range(2):
                pool.wait_ge(y_stored[par], 16 * (TT // 2))

        @block.scalar
        def _(act):
            act.wait_ge(s["logp_in"], 1)
            act.activation(logp[:], lbias[:, 1], ACT.Ln).then_inc(s["logp_ready"], 1)

            def xT(t, q):
                for h in range(2):
                    act.wait_ge(s["transposed"], 2 * t + h + 1)
                    if h == 0:
                        wait(act, s["y_done"], NH * (t - 1))
                    act.activation(xT_hi[:, q % 2, 4 * h:4 * h + 4], tp[:, h], ACT.Copy).then_inc(s["xT_hi_ready"], 1)

            xT(0, 0)
            act.wait_ge(s["az_loaded"], 32 * E_ACT)
            act.activation(az_hi[:, :, 0:ER], a_raw[:], ACT.Copy)
            act.activation(az_hi[:, :, ER:Z], r_raw[:].rearrange("p e c -> p c e"), ACT.Copy).then_inc(s["az_split_hi"], 1)
            for i in range(DC // 2):
                act.wait_ge(w_loaded[i % 2], 16 * (i // 2 + 1))
                act.activation(w_hi[:, 2 * i:2 * i + 2], w_raw[:, i % 2], ACT.Copy).then_inc(s["w_hi_ready"], 1)
                if i == 1:
                    act.wait_ge(s["b_loaded"], 16 * (E_ACT + 1))
                    act.activation(b_hi[:], b_raw[:], ACT.Copy).then_inc(s["b_split_hi"], 1)

            def tile(t, q):
                act.wait_ge(s["max_ready"], t + 1)
                act.activation(expl[:], logit[:], ACT.Exp, bias=negmax[:], accum_out=esum[:]).then_inc(s["exp_ready"], 1)
                act.wait_ge(s["azT_done"], t + 1)
                wait(act, s["y_done"], NH * (t - 1))
                act.activation(azsT[:, q % 2], ap[0:KB, 0:P], ACT.Copy).then_inc(s["azsT_ready"], 1)
                if not is_last(t):
                    xT(t + 1, (q + 1) % 4)

            tiles(act, tile)

        @block.vector
        def _(dve):
            def statistics(t, q):
                par = q % 2
                dve.wait_ge(x_loaded[q], 16 * ((t - q) // 4 + 1) if isinstance(t, int) else 4 * (t - q) + 16)
                wait(dve, s["mv_done"], t - 1)
                dve.bn_stats(stats[:, par, 0], x1t[:, q, 0:DM // 2])
                dve.bn_stats(stats[:, par, 1], x1t[:, q, DM // 2:DM]).then_inc(s["stats_done"], 1)

            def variance(t, q):
                par = q % 2
                dve.bn_aggr(mv[:, par], stats[:, par]).then_inc(s["mv_done"], 1)
                dve.wait_ge(s["mv_done"], t + 1)
                dve.tensor_scalar(vareps[:, par], mv[:, par, 1:2], EPS, None, ALU.add).then_inc(s["var_ready"], 1)

            def scale(t, q):
                par = q % 2
                dve.wait_ge(s["rstd_ready"], t + 1)
                wait(dve, s["transposed"], 2 * (t - 1))
                dve.tensor_scalar(xn[:, par], x1t[:, q], mv[:, par, 0:1], rstd[:, par], ALU.subtract, ALU.mult).then_inc(s["xn_ready"], 1)

            def xT_low(t, q):
                for h in range(2):
                    dve.wait_ge(s["xT_hi_ready"], 2 * t + h + 1)
                    dve.tensor_tensor(xT_lo[:, q % 2, 4 * h:4 * h + 4], tp[:, h], xT_hi[:, q % 2, 4 * h:4 * h + 4], ALU.subtract).then_inc(s["xT_lo_ready"], 1)

            def gate(t, q):
                par = q % 2
                if not is_last(t):
                    dve.wait_ge(s["stats_done"], t + 2)
                dve.wait_ge(s["z_done"], t + 1)
                wait(dve, s["exp_ready"], t)
                dve.tensor_tensor(logit[:], zp[:, ER:Z], lsum[:], ALU.add).then_inc(s["logit_ready"], 1)
                if not is_last(t):
                    variance(t + 1, (q + 1) % 4)
                dve.wait_ge(s["logit_ready"], t + 1)
                dve.tensor_reduce(negmax[:], logit[:], AX_X, ALU.max, negate=True).then_inc(s["max_ready"], 1)
                dve.wait_ge(s["exp_ready"], t + 1)
                dve.reciprocal(erec[:], esum[:]).then_inc(s["rec_ready"], 1)
                dve.wait_ge(s["rec_ready"], t + 1)
                dve.tensor_scalar(alpha[:], expl[:], erec[:], LORA_SCALE, ALU.mult, ALU.mult).then_inc(s["alpha_ready"], 1)
                dve.wait_ge(s["alpha_ready"], t + 1)
                dve.tensor_tensor(az[:].rearrange("p (e r) -> p e r", r=RANK), zp[:, 0:ER].rearrange("p (e r) -> p e r", r=RANK),
                                  alpha[:].unsqueeze(2).to_broadcast([P, E_ACT, RANK]), ALU.mult).then_inc(s["az_ready"], 1)
                dve.wait_ge(s["az_ready"], t + 1)
                wait(dve, s["azT_done"], t - 1)
                dve.tensor_copy(azs[:, par, 0:ER], az[:]).then_inc(s["azs_hi_ready"], 1)
                dve.tensor_copy(azs[:, par, 2 * ER:3 * ER], az[:])
                dve.wait_ge(s["azs_hi_ready"], t + 1)
                dve.tensor_tensor(azs[:, par, ER:2 * ER], az[:], azs[:, par, 0:ER], ALU.subtract).then_inc(s["azs_ready"], 1)

            def outputs(t, q, h):
                dve.wait_ge(s["y_done"], NH * t + h + 1)
                if h == 0:
                    if isinstance(t, int):
                        wait(dve, y_stored[q % 2], 16 * (t // 2))
                    else:
                        dve.wait_ge(y_stored[q % 2], 8 * (t - q % 2))
                dve.tensor_tensor(y[:, q % 2, h * BANK:(h + 1) * BANK], yp[:, q % 2, h], x1t[:, q, h * BANK:(h + 1) * BANK], ALU.add).then_inc(s["y_ready"], 1)

            dve.memset(azs[:, :, 3 * ER:KB].bitcast(F32), 1.0).then_inc(s["ones_ready"], 1)
            statistics(0, 0)
            dve.wait_ge(s["stats_done"], 1)
            variance(0, 0)
            scale(0, 0)
            dve.wait_ge(s["lbias_loaded"], 32 * E_ACT)
            dve.tensor_scalar(lbias[:, 1], lbias[:, 1], PRIOR_EPS, None, ALU.add).then_inc(s["logp_in"], 1)
            xT_low(0, 0)
            dve.wait_ge(s["logp_ready"], 1)
            dve.tensor_tensor(lsum[:], logp[:], lbias[:, 0], ALU.add).then_inc(s["lsum_ready"], 1)
            dve.wait_ge(s["az_split_hi"], 1)
            dve.tensor_tensor(az_lo[:, :, 0:ER], a_raw[:], az_hi[:, :, 0:ER], ALU.subtract)
            dve.tensor_tensor(az_lo[:, :, ER:Z], r_raw[:].rearrange("p e c -> p c e"), az_hi[:, :, ER:Z], ALU.subtract).then_inc(s["az_split_lo"], 1)
            for i in range(DC // 2):
                dve.wait_ge(s["w_hi_ready"], i + 1)
                dve.tensor_tensor(w_lo[:, 2 * i:2 * i + 2], w_raw[:, i % 2], w_hi[:, 2 * i:2 * i + 2], ALU.subtract).then_inc(s["w_lo_ready"], 1)
                if i == 1:
                    dve.wait_ge(s["b_split_hi"], 1)
                    dve.tensor_tensor(b_lo[:], b_raw[:], b_hi[:], ALU.subtract).then_inc(s["b_split_lo"], 1)
            dve.wait_ge(s["lsum_ready"], 1)

            def tile(t, q):
                if not is_last(t):
                    statistics(t + 1, (q + 1) % 4)
                gate(t, q)
                if not is_last(t):
                    scale(t + 1, (q + 1) % 4)
                    xT_low(t + 1, (q + 1) % 4)
                for h in range(NH):
                    outputs(t, q, h)

            tiles(dve, tile)

        @block.tensor
        def _(pe):
            def transposes(t, q):
                pe.wait_ge(s["xn_ready"], t + 1)
                for h in range(2):
                    wait(pe, s["xT_lo_ready"], 2 * (t - 1) + h + 1)
                    for c in range(4 * h, 4 * h + 4):
                        tr = pe.transpose(tp[:, h, (c % 4) * P:(c % 4 + 1) * P], xn[:, q % 2, c * P:(c + 1) * P], ident[:])
                    tr.then_inc(s["transposed"], 1)

            def dense(t, q, h):
                if h == 0:
                    wait(pe, s["y_ready"], NH * (t - 1))
                for c in range(DC):
                    if isinstance(t, int) and t == 0 and h == 0 and c % 2 == 0:
                        pe.wait_ge(s["w_lo_ready"], c // 2 + 1)
                    three_pass(pe, yp[:, q % 2, h], xT_hi[:, q % 2, c], xT_lo[:, q % 2, c],
                               w_hi[:, c, h * BANK:(h + 1) * BANK], w_lo[:, c, h * BANK:(h + 1) * BANK], c == 0, False)

            def tile(t, q):
                if isinstance(t, int) and t == 0:
                    transposes(0, 0)
                    pe.wait_ge(s["az_split_lo"], 1)
                pe.wait_ge(s["xT_lo_ready"], 2 * (t + 1))
                wait(pe, s["az_ready"], t)
                for c in range(DC):
                    z = three_pass(pe, zp[:, 0:Z], xT_hi[:, q % 2, c], xT_lo[:, q % 2, c], az_hi[:, c], az_lo[:, c], c == 0, c == DC - 1)
                z.then_inc(s["z_done"], 1)
                dense(t, q, 0)
                if isinstance(t, int) and t == 0:
                    pe.wait_ge(s["ones_ready"], 1)
                    pe.wait_ge(s["b_stacked"], 16 * 5)
                pe.wait_ge(s["azs_ready"], t + 1)
                wait(pe, s["azsT_ready"], t)
                pe.transpose(ap[0:KB, 0:P], azs[:, q % 2].bitcast(F32), ident[:]).then_inc(s["azT_done"], 1)
                if not is_last(t):
                    transposes(t + 1, (q + 1) % 4)
                dense(t, q, 1)
                pe.wait_ge(s["azsT_ready"], t + 1)
                for h in range(NH):
                    pe.matmul(yp[:, q % 2, h], azsT[:, q % 2], b_stack[:, h * BANK:(h + 1) * BANK], start=False, stop=True).then_inc(s["y_done"], 1)

            tiles(pe, tile)


def program(nc, x, conv_w, conv_b, wq, wk, wv, wo, pw, bq, bk, bv, bo, pb, w_base, b_base, lora_a, lora_b, router_w, router_b,
            prior, active, c_dram, x1_dram, out):
    with nc.sbuf_tensor("ident", [P, P], F32) as ident:
        with nc.semaphore("ident_zero") as ident_zero, nc.semaphore("ident_ready") as ident_ready, nc.Block() as block:
            @block.gpsimd
            def _(pool):
                pool.memset(ident[:], 0.0).then_inc(ident_zero, 1)
                pool.wait_ge(ident_zero, 1)
                pool.affine_select(out=ident[:], in_=ident[:], compare_op=ALU.not_equal, fill=1.0, base=0,
                                   pattern=[[-1, P]], channel_multiplier=1).then_inc(ident_ready, 1)
                pool.wait_ge(ident_ready, 1)
        conv_phase(nc, x, conv_w, c_dram, ident)
        attention_phase(nc, x, c_dram, conv_b, wq, wk, wv, wo, pw, bq, bk, bv, bo, pb, x1_dram, ident)
        ffn_phase(nc, x1_dram.rearrange("n l d -> (n l) d"), w_base, b_base, lora_a, lora_b, router_w, router_b, prior, active,
                  out.rearrange("n l d -> (n l) d"), ident)


def kernel(**inputs):
    import numpy as np
    import concourse.bacc as bacc
    from concourse.bass_utils import run_bass_kernel_spmd

    attn = {k[len("L0_attn_"):]: np.asarray(v) for k, v in inputs.items() if k.startswith("L0_attn_")}
    ffn = {k[len("L0_ffn_"):]: np.asarray(v) for k, v in inputs.items() if k.startswith("L0_ffn_")}
    rows = lambda a: a.reshape(-1, P, a.shape[-1]).transpose(1, 0, 2)
    column = lambda a: a.reshape(-1, P).T
    laid_out = {
        "x": attn["inputs"],
        "conv_w": attn["conv_w"].reshape(3, DC, P, MC, P).transpose(3, 2, 1, 0, 4),
        "conv_b": column(attn["conv_b"]),
        "wq": rows(attn["wq"].reshape(W, HW_)), "wk": rows(attn["wk"].reshape(W, HW_)), "wv": rows(attn["wv"].reshape(W, HW_)),
        "wo": rows(attn["wo"].reshape(HW_, W)), "pw": rows(attn["proj_w"]),
        "bq": column(attn["bq"]), "bk": column(attn["bk"]), "bv": column(attn["bv"]), "bo": column(attn["bo"]),
        "pb": attn["proj_b"].reshape(1, DM),
        "w_base": rows(ffn["W_base"].T), "b_base": ffn["b_base"].reshape(1, DM),
        "lora_a": ffn["lora_A"].reshape(E_TOT, RANK, DC, P).transpose(0, 3, 2, 1),
        "lora_b": ffn["lora_B"].transpose(0, 2, 1),
        "router_w": ffn["router_W"].reshape(E_TOT, DC, P).transpose(0, 2, 1),
        "router_b": ffn["router_b"].reshape(E_TOT, 1), "prior": ffn["domain_prior"].reshape(E_TOT, 1),
        "active": ffn["active"].reshape(1, E_ACT),
    }
    nc = bacc.Bacc("TRN2", target_bir_lowering=False, num_devices=1)
    arrays, args = {}, []
    for name, a in laid_out.items():
        a = np.ascontiguousarray(a)
        arrays[f"in_{name}"] = a
        args.append(nc.dram_tensor(f"in_{name}", a.shape, mybir.dt.from_np(a.dtype), kind="ExternalInput").ap())
    c_dram = nc.dram_tensor("c_scratch", (N, MC, P, L), F32, kind="Internal").ap()
    x1_dram = nc.dram_tensor("x1_scratch", (N, L, DM), F32, kind="Internal").ap()
    out = nc.dram_tensor("out_0", (N, L, DM), F32, kind="ExternalOutput").ap()
    program(nc, *args, c_dram, x1_dram, out)
    return run_bass_kernel_spmd(nc, [arrays], core_ids=[0]).results[0]["out_0"]
```

```python
import math
from contextlib import ExitStack

import concourse.bass as bass
from concourse import mybir

F32 = mybir.dt.float32
F32R = mybir.dt.float32r
I32 = mybir.dt.int32
ALU = mybir.AluOpType
ACT = mybir.ActivationFunctionType
AX_X = mybir.AxisListType.X

P = 128
N, L, DM = 2, 1024, 1024
W, H, DH = 256, 16, 64
TOK = N * L
DC = DM // P
MC = 3 * W // P
WC = W // P
LT = L // P
PAIRS = L // 2
NV = 4
EPS = 1e-5
HW_ = H * DH
GB = 2
GT = GB * P
BANK = 512

E_TOT, E_ACT, RANK = 16, 4, 8
ER = E_ACT * RANK
PRIOR_EPS = 1e-12
LORA_SCALE = 16.0 / 8.0
MASKED = -1e30


def wait(eng, sem, count):
    if isinstance(count, int) and count <= 0:
        return
    eng.wait_ge(sem, count)


class Space:

    def __init__(self, nc, ctx, prefix):
        self.nc, self.ctx, self.prefix = nc, ctx, prefix

    def sb(self, name, shape, dtype=F32):
        return self.ctx.enter_context(self.nc.sbuf_tensor(f"{self.prefix}_{name}", shape, dtype))

    def ps(self, name, shape):
        return self.ctx.enter_context(self.nc.psum_tensor(f"{self.prefix}_{name}", shape, F32))

    def sem(self, name):
        return self.ctx.enter_context(self.nc.semaphore(f"{self.prefix}_{name}"))


def three_pass(pe, out, w_hi, w_lo, x_hi, x_lo, first, last):
    pe.matmul(out, w_hi, x_hi, start=first, stop=False)
    pe.matmul(out, w_hi, x_lo, start=False, stop=False)
    return pe.matmul(out, w_lo, x_hi, start=False, stop=last)


def size_of(shape):
    return -(-4 * math.prod(shape[1:]) // 32) * 32


def place(nc, offset, tensors):
    out = []
    for name, shape, dtype in tensors:
        out.append(nc.alloc_sbuf_tensor_at(name, shape, dtype, offset=offset))
        offset += size_of(shape)
    return out


class SharedArea:

    INPUT = (("xn", [P, LT, DM], F32),
             ("xT", [P, 2, L + 2], F32),
             ("u", [P, NV, PAIRS], F32))
    START = (("wqk_hi", [P, 2, WC, HW_], F32R),
             ("wqk_lo", [P, 2, WC, HW_], F32R),
             ("c_raw", [P, MC, GT], F32),
             ("c0_hi", [P, MC, GT], F32R),
             ("cb_c", [P, MC], F32),
             ("bqk_c", [P, 2, HW_ // P], F32), ("bv_c", [P, HW_ // P], F32), ("bo_c", [P, WC], F32))
    SIZE = max(sum(size_of(shape) // 4 for _, shape, _ in part) for part in (INPUT, START))

    def __init__(self, nc, offset):
        self.xn, self.xT, self.u = place(nc, offset, self.INPUT)
        self.start = place(nc, offset, self.START)
        self.wqk_raw, = place(nc, offset + size_of([P, 2, WC, HW_]), (("wqk_raw", [P, 2, WC, HW_], F32),))


def conv_phase(nc, x, conv_w, c_dram, c_stored, ident, shared, wq, wk, conv_b, bq, bk, bv, bo):
    with ExitStack() as ctx:
        sp = Space(nc, ctx, "conv")
        xn, xT, u = shared.xn, shared.xT, shared.u
        x_hi = sp.sb("x_hi", [P, DC, NV, PAIRS], F32R)
        x_lo = sp.sb("x_lo", [P, DC, NV, PAIRS], F32R)
        WR, RR = 4, 4
        raw = sp.sb("raw", [P, RR, 3, P])
        wsum = sp.sb("wsum", [P, 2, P])
        wmix = sp.sb("wmix", [P, 2, 2, P])
        w_hi = sp.sb("w_hi", [P, WR, NV, P], F32R)
        w_lo = sp.sb("w_lo", [P, WR, NV, P], F32R)
        p1 = sp.sb("p1", [P, PAIRS])
        y = sp.sb("y", [P, PAIRS, 2])
        stats = sp.sb("stats", [P, 2, 6])
        mv = sp.sb("mv", [P, LT, 2])
        vareps = sp.sb("vareps", [P, LT])
        rstd = sp.sb("rstd", [P, LT])
        mhalf = sp.sb("mhalf", [P, 1])

        acc = [sp.ps("acc_even", [P, NV, BANK]), sp.ps("acc_odd", [P, NV, BANK])]
        Q0, Q3, Q1, Q2 = 0, 1, 2, 3

        x_loaded = [sp.sem(f"x_loaded{j}") for j in range(LT)]
        raw_loaded = [sp.sem(f"raw_loaded{i}") for i in range(RR)]
        names = ("power_ready", "pads_ready", "stats_done", "mv_done", "var_ready", "rstd_ready", "xn_ready", "transposed", "xT_ready", "u01_ready", "u23_ready",
                 "x_hi_ready", "x_lo_ready", "wsum_ready", "wmix_ready", "w_hi_ready", "w_lo_ready", "unit_done",
                 "p1_ready", "mixed", "y_ready", "qk_w_loaded", "early_loaded", "qk_w_hi_ready", "qk_w_lo_ready", "c0_sum_ready", "c0_hi_ready")
        s = {n: sp.sem(n) for n in names}
        s["y_stored"] = c_stored
        wqk_hi, wqk_lo, c0_raw, c0_hi, cb_c, bqk_c, bv_c, bo_c = shared.start
        EARLY_LOADS = 6
        block = ctx.enter_context(nc.Block())

        EVAC_AT = WR

        def before(n, m, st, store):
            if not isinstance(m, int):
                store(n, m - 1, st - 1)
            elif m:
                store(n, m - 1, st - 1)
            elif n:
                store(n - 1, MC - 1, st - 1)

        def steps(eng, n, one_step):
            straight = (0, 1) if n == N - 1 else (0, 1, MC - 2, MC - 1)
            for m in straight[:2]:
                one_step(n, m, m % 2, MC * n + m)
            with eng.Fori(1, (MC - len(straight[2:])) // 2) as k:
                for par in range(2):
                    one_step(n, 2 * k + par, par, 2 * k + (MC * n + par))
            for m in straight[2:]:
                one_step(n, m, m % 2, MC * n + m)

        EARLY = DC - EVAC_AT

        def known(m):
            return isinstance(m, int)

        def chunk_at(n, m, c):
            if known(m) and m == 0 and (n == 0 or c >= EARLY):
                return n, c, c == (0 if n == 0 else EARLY), c == DC - 1
            if known(m) and m == MC - 1 and n + 1 < N and c >= EVAC_AT:
                return n + 1, c - EVAC_AT, c == EVAC_AT, c == DC - 1
            return None

        def normalises(n, m):
            return known(m) and m == 1 and n + 1 < N

        def turned(n, c):
            return acc[0 if n and c < EARLY else 1][:, 2 * (c % 2):2 * (c % 2) + 2, :]

        def winograd_input(eng, c, v):
            d = [xT[:, c % 2, a:a + 2 * PAIRS - 1:2] for a in range(4)]
            a, b, op = ((d[0], d[2], ALU.subtract), (d[3], d[1], ALU.subtract), (d[1], d[2], ALU.add), (d[2], d[1], ALU.subtract))[v]
            return eng.tensor_tensor(u[:, v], a, b, op)

        @block.sync
        def _(sync):
            def load_x(n, j):
                sync.dma_start(xn[:, j], x[n, j * P:(j + 1) * P, :]).then_inc(x_loaded[j], 16)

            def load_early():
                sync.wait_ge(s["transposed"], DC * N)
                for k, w in enumerate((wq, wk)):
                    sync.dma_start(shared.wqk_raw[:, k], w).then_inc(s["qk_w_loaded"], 16)
                sync.wait_ge(s["x_lo_ready"], NV * DC * N)
                sync.wait_ge(s["u23_ready"], 2 * DC * N)
                sync.wait_ge(s["y_stored"], 16 * MC)
                sync.dma_start(c0_raw[:], c_dram[:, :, 0:GT].rearrange("m p l -> p m l")).then_inc(s["early_loaded"], 16)
                for dst, src in ((cb_c[:], conv_b), (bqk_c[:, 0], bq), (bqk_c[:, 1], bk), (bv_c[:], bv), (bo_c[:], bo)):
                    sync.dma_start(dst, src).then_inc(s["early_loaded"], 16)

            def load_step(n, m, par, st):
                for c in range(DC):
                    unit = DC * st + c
                    if normalises(n, m):
                        if c == 0:
                            sync.wait_ge(s["transposed"], DC * (n + 1))
                        load_x(n + 1, c)
                    wait(sync, s["w_lo_ready"], unit - RR + 1)
                    if known(m) and m == 1 and n == N - 1 and c == DC - 1:
                        load_early()
                    sync.dma_start(raw[:, c % RR], conv_w[bass.ds(m, 1), :, c].rearrange("m p t o -> p (m t) o")).then_inc(raw_loaded[c % RR], 16)

            for j in range(LT):
                load_x(0, j)
            for n in range(N):
                steps(sync, n, load_step)

        @block.gpsimd
        def _(pool):
            pool.memset(mhalf[:], -0.5).then_inc(s["power_ready"], 1)

            def store(n, m, st):
                pool.wait_ge(s["y_ready"], st + 1)
                pool.dma_start(c_dram[bass.ds(m, 1), :, n * L:(n + 1) * L].rearrange("m p l -> p (m l)"), y[:].rearrange("p i k -> p (i k)")).then_inc(s["y_stored"], 16)

            def step(n, m, par, st):
                for c in range(DC):
                    unit = DC * st + c
                    if c == EVAC_AT:
                        before(n, m, st, store)
                    wait(pool, raw_loaded[c % RR], 16 * (DC // RR * st + c // RR + 1))
                    wait(pool, s["wmix_ready"], unit - 1)
                    pool.tensor_tensor(wsum[:, c % 2], raw[:, c % RR, 0], raw[:, c % RR, 2], ALU.add).then_inc(s["wsum_ready"], 1)
                    pool.wait_ge(s["wsum_ready"], unit + 1)
                    wait(pool, s["w_lo_ready"], unit - 1)
                    pool.tensor_tensor(wmix[:, c % 2, 0], wsum[:, c % 2], raw[:, c % RR, 1], ALU.add)
                    pool.tensor_tensor(wmix[:, c % 2, 1], wsum[:, c % 2], raw[:, c % RR, 1], ALU.subtract).then_inc(s["wmix_ready"], 1)
                    if normalises(n, m):
                        power(n + 1, c)
                    chunk = chunk_at(n, m, c)
                    if chunk:
                        for v in (2, 3):
                            k = DC * chunk[0] + chunk[1]
                            pool.wait_ge(s["xT_ready"], k + 1)
                            wait(pool, s["x_lo_ready"], NV * (k - 1) + v + 1)
                            winograd_input(pool, chunk[1], v).then_inc(s["u23_ready"], 1)

            def power(n, j):
                pool.wait_ge(s["var_ready"], LT * n + j + 1)
                pool.tensor_tensor(rstd[:, j:j + 1], vareps[:, j:j + 1], mhalf[:], ALU.pow).then_inc(s["rstd_ready"], 1)

            pool.wait_ge(s["power_ready"], 1)
            for j in range(LT):
                power(0, j)
            for n in range(N):
                steps(pool, n, step)
            pool.wait_ge(s["early_loaded"], 16 * EARLY_LOADS)
            for i in range(MC):
                pool.tensor_tensor(c0_raw[:, i], c0_raw[:, i], cb_c[:, i:i + 1].to_broadcast([P, GT]), ALU.add).then_inc(s["c0_sum_ready"], 1)
            store(N - 1, MC - 1, MC * N - 1)

        @block.scalar
        def _(act):
            def chunk_out(n, c):
                k = DC * n + c
                act.wait_ge(s["transposed"], k + 1)
                wait(act, s["u01_ready"], 2 * (k - 1))
                wait(act, s["u23_ready"], 2 * (k - 1))
                act.activation(xT[:, c % 2, 1:L + 1], turned(n, c), ACT.Copy).then_inc(s["xT_ready"], 1)

            def high_input(n, c, v):
                k = DC * n + c
                act.wait_ge(s["u23_ready" if v >= 2 else "u01_ready"], 2 * k + v % 2 + 1)
                if n:
                    act.wait_ge(s["unit_done"], DC * (MC * n - 1) + c + 1)
                act.activation(x_hi[:, c, v], u[:, v], ACT.Copy).then_inc(s["x_hi_ready"], 1)

            def evacuate(st, par):
                act.wait_ge(s["unit_done"], DC * st + DC)
                wait(act, s["mixed"], st)
                act.activation(p1[:], acc[par][:, Q1, :], ACT.Copy).then_inc(s["p1_ready"], 1)

            def step(n, m, par, st):
                for c in range(DC):
                    unit = DC * st + c
                    if c == EVAC_AT and not (known(st) and st == 0):
                        evacuate(st - 1, 1 - par)
                    chunk = chunk_at(n, m, c)
                    if chunk:
                        cn, cc, starts, ends = chunk
                        if starts:
                            chunk_out(cn, cc)
                        high_input(cn, cc, 0)
                        high_input(cn, cc, 1)
                    wait(act, s["unit_done"], unit - WR + 1)
                    act.wait_ge(raw_loaded[c % RR], 16 * (DC // RR * st + c // RR + 1))
                    act.activation(w_hi[:, c % WR, 0:2], raw[:, c % RR, 0:3:2], ACT.Copy)
                    act.wait_ge(s["wmix_ready"], unit + 1)
                    act.activation(w_hi[:, c % WR, 2:4], wmix[:, c % 2], ACT.Copy, scale=0.5).then_inc(s["w_hi_ready"], 1)
                    if chunk:
                        if not ends:
                            chunk_out(cn, cc + 1)
                        high_input(cn, cc, 2)
                        high_input(cn, cc, 3)

            for n in range(N):
                steps(act, n, step)
            for i in range(2):
                act.wait_ge(s["qk_w_loaded"], 16 * 2)
                act.activation(wqk_hi[:, i], shared.wqk_raw[:, i], ACT.Copy).then_inc(s["qk_w_hi_ready"], 1)
            for i in range(MC):
                act.wait_ge(s["c0_sum_ready"], i + 1)
                act.activation(c0_hi[:, i], c0_raw[:, i], ACT.Copy).then_inc(s["c0_hi_ready"], 1)
            evacuate(MC * N - 1, 1)

        @block.vector
        def _(dve):
            dve.memset(xT[:, :, 0:1], 0.0).then_inc(s["pads_ready"], 1)
            dve.memset(xT[:, :, L + 1:L + 2], 0.0).then_inc(s["pads_ready"], 1)

            def statistics(n, j):
                k = LT * n + j
                dve.wait_ge(x_loaded[j], 16 * (n + 1))
                wait(dve, s["mv_done"], k)
                dve.bn_stats(stats[:, 0], xn[:, j, 0:DM // 2])
                dve.bn_stats(stats[:, 1], xn[:, j, DM // 2:DM]).then_inc(s["stats_done"], 1)
                dve.wait_ge(s["stats_done"], k + 1)
                dve.bn_aggr(mv[:, j], stats[:]).then_inc(s["mv_done"], 1)
                dve.wait_ge(s["mv_done"], k + 1)
                dve.tensor_scalar(vareps[:, j:j + 1], mv[:, j, 1:2], EPS, None, ALU.add).then_inc(s["var_ready"], 1)

            def scale(n, j):
                dve.wait_ge(s["rstd_ready"], LT * n + j + 1)
                dve.tensor_scalar(xn[:, j], xn[:, j], mv[:, j, 0:1], rstd[:, j:j + 1], ALU.subtract, ALU.mult).then_inc(s["xn_ready"], 1)

            def normalise(n, j):
                statistics(n, j)
                if j:
                    scale(n, j - 1)
                if j == LT - 1:
                    scale(n, j)

            def low_input(n, c, v):
                dve.wait_ge(s["x_hi_ready"], NV * (DC * n + c) + v + 1)
                dve.tensor_tensor(x_lo[:, c, v], u[:, v], x_hi[:, c, v], ALU.subtract).then_inc(s["x_lo_ready"], 1)

            def outputs(st, par):
                dve.wait_ge(s["p1_ready"], st + 1)
                wait(dve, s["y_stored"], 16 * st)
                dve.tensor_tensor(y[:, :, 0], acc[par][:, Q2, :], p1[:], ALU.add)
                dve.tensor_tensor(y[:, :, 1], p1[:], acc[par][:, Q2, :], ALU.subtract).then_inc(s["mixed"], 1)
                dve.wait_ge(s["mixed"], st + 1)
                dve.tensor_tensor(y[:, :, 0], acc[par][:, Q0, :], y[:, :, 0], ALU.add)
                dve.tensor_tensor(y[:, :, 1], acc[par][:, Q3, :], y[:, :, 1], ALU.add).then_inc(s["y_ready"], 1)

            def step(n, m, par, st):
                for c in range(DC):
                    unit = DC * st + c
                    if c == EVAC_AT and not (known(st) and st == 0):
                        outputs(st - 1, 1 - par)
                    if normalises(n, m):
                        normalise(n + 1, c)
                    chunk = chunk_at(n, m, c)
                    if chunk:
                        cn, cc, starts, ends = chunk
                        k = DC * cn + cc
                        if k == 0:
                            dve.wait_ge(s["pads_ready"], 2)
                        dve.wait_ge(s["xT_ready"], k + 1)
                        for v in (0, 1):
                            wait(dve, s["x_lo_ready"], NV * (k - 1) + v + 1)
                            winograd_input(dve, cc, v).then_inc(s["u01_ready"], 1)
                        if not starts:
                            low_input(cn, cc - 1, 2)
                            low_input(cn, cc - 1, 3)
                        low_input(cn, cc, 0)
                    dve.wait_ge(s["w_hi_ready"], unit + 1)
                    dve.tensor_tensor(w_lo[:, c % WR, 0:2], raw[:, c % RR, 0:3:2], w_hi[:, c % WR, 0:2], ALU.subtract)
                    dve.scalar_tensor_tensor(w_lo[:, c % WR, 2:4], wmix[:, c % 2], 0.5, w_hi[:, c % WR, 2:4], ALU.mult, ALU.subtract).then_inc(s["w_lo_ready"], 1)
                    if chunk:
                        low_input(cn, cc, 1)
                        if ends:
                            low_input(cn, cc, 2)
                            low_input(cn, cc, 3)

            for j in range(LT):
                normalise(0, j)
            for n in range(N):
                steps(dve, n, step)
            for i in range(2):
                dve.wait_ge(s["qk_w_hi_ready"], i + 1)
                dve.tensor_tensor(wqk_lo[:, i], shared.wqk_raw[:, i], wqk_hi[:, i], ALU.subtract).then_inc(s["qk_w_lo_ready"], 1)
            outputs(MC * N - 1, 1)

        @block.tensor
        def _(pe):
            def transpose_chunk(n, c):
                k = DC * n + c
                if n and c in (0, EARLY):
                    pe.wait_ge(s["y_ready"], MC * n - (1 if c == 0 else 0))
                elif c >= 2:
                    pe.wait_ge(s["xT_ready"], k - 1)
                for j in range(LT):
                    if c == 0:
                        pe.wait_ge(s["xn_ready"], LT * n + j + 1)
                    o = turned(n, c)[:, j // 4, (j % 4) * P:(j % 4 + 1) * P]
                    t = pe.transpose(o, xn[:, j, c * P:(c + 1) * P], ident[:])
                t.then_inc(s["transposed"], 1)

            def step(n, m, par, st):
                if known(m) and m < 2:
                    wait(pe, s["xT_ready"], DC * n + (DC if m else EARLY if n else 0))
                if not (known(m) and m == 1):
                    wait(pe, s["y_ready"], st - 1)
                if known(st) and st == 0:
                    transpose_chunk(0, 0)
                    transpose_chunk(0, 1)
                for c in range(DC):
                    unit = DC * st + c
                    later = chunk_at(n, m, c + 2)
                    if later and c + 2 < DC:
                        transpose_chunk(later[0], later[1])
                    pe.wait_ge(s["w_lo_ready"], unit + 1)
                    for v in range(NV):
                        if known(m) and m == 0:
                            pe.wait_ge(s["x_lo_ready"], NV * (DC * n + c) + v + 1)
                        mm = three_pass(pe, acc[par][:, v, :], w_hi[:, c % WR, v], w_lo[:, c % WR, v],
                                        x_hi[:, c, v], x_lo[:, c, v], c == 0, c == DC - 1)
                    mm.then_inc(s["unit_done"], 1)

            for n in range(N):
                steps(pe, n, step)


def attention_phase(nc, x, c_dram, c_stored, wv, wo, pw, pb, x1, x1_stored, ident, shared):
    NG = TOK // GT
    NP = H // 2
    NJ = NP * NG
    UN = 2 * GB
    OC = HW_ // P
    VT = GB * HW_ // BANK
    YT = GB * DM // BANK
    SC, NRM, TR, PV, OT = 2, 3, 4, 5, 6
    with ExitStack() as ctx:
        sp = Space(nc, ctx, "attn")
        stage = sp.sb("stage", [P, 2, DM])
        xr = stage
        wqk_hi, wqk_lo, c_raw, c0_hi, cb_c, bqk_c, bv_c, bo_c = shared.start
        wv_hi = sp.sb("wv_hi", [P, WC, HW_], F32R)
        wv_lo = sp.sb("wv_lo", [P, WC, HW_], F32R)
        wo_hi = sp.sb("wo_hi", [P, OC, W], F32R)
        wo_lo = sp.sb("wo_lo", [P, OC, W], F32R)
        pw_hi = sp.sb("pw_hi", [P, WC, DM], F32R)
        pw_lo = sp.sb("pw_lo", [P, WC, DM], F32R)
        ba_c = sp.sb("ba_c", [P, WC])
        pb_r = sp.sb("pb_r", [P, DM])
        mask = sp.sb("mask", [P, P])
        c_hi = (c0_hi, sp.sb("c_hi", [P, MC, GT], F32R))
        c_lo = sp.sb("c_lo", [P, 2, MC, GT], F32R)
        v_hi = sp.sb("v_hi", [P, GB, HW_], F32R)
        v_lo = sp.sb("v_lo", [P, GB, HW_], F32R)
        q_hi = sp.sb("q_hi", [P, 2, GT], F32R)
        q_lo = sp.sb("q_lo", [P, 2, GT], F32R)
        k_hi = sp.sb("k_hi", [P, 2, GB, 2, P], F32R)
        k_lo = sp.sb("k_lo", [P, 2, GB, 2, P], F32R)
        pr = sp.sb("pr", [P, 4, UN, P])
        negmax = sp.sb("negmax", [P, 2, UN])
        rsum = sp.sb("rsum", [P, 2, UN])
        rrec = sp.sb("rrec", [P, 4, UN])
        pT_hi = sp.sb("pT_hi", [P, 2, GB, 2 * P], F32R)
        pT_lo = sp.sb("pT_lo", [P, 2, GB, 2 * P], F32R)
        oT_hi = sp.sb("oT_hi", [P, 2, OC, GT], F32R)
        oT_lo = sp.sb("oT_lo", [P, 2, OC, GT], F32R)
        a_hi = sp.sb("a_hi", [P, WC, GT], F32R)
        a_lo = sp.sb("a_lo", [P, WC, GT], F32R)

        qkp = sp.ps("qkp", [P, 2, 2, GT])
        scp = sp.ps("scp", [P, GB, 2 * P])
        ptp = sp.ps("ptp", [P, GB, 2 * P])
        op = sp.ps("op", [P, GB, 2, P])
        gp = sp.ps("gp", [P, 3, BANK])

        names = ("x_loaded", "pb_loaded", "c_loaded", "w_hi_ready", "w_lo_ready", "bvo_done", "ba_part", "ba_ready",
                 "mask0", "mask_ready", "k_hi_zero", "k_lo_zero", "c0_lo_ready", "c_sum_ready", "c_hi_ready", "c_lo_ready", "v_done", "v_hi_ready", "v_lo_ready",
                 "qk_done", "qk_hi_ready", "qk_lo_ready", "sc_done", "max_ready", "exp_ready", "rrec_ready", "p_ready",
                 "pT_done", "pT_hi_ready", "pT_lo_ready", "o_done", "oT_hi_ready", "oT_lo_ready",
                 "a_done", "a_hi_ready", "a_lo_ready", "xb_ready", "y_done", "x1_ready")
        s = {n: sp.sem(n) for n in names}
        w_loaded = [sp.sem(f"w_loaded{i}") for i in range(2)]
        block = ctx.enter_context(nc.Block())

        pieces = [(wv[:, i], wv_hi[:, i], wv_lo[:, i]) for i in range(WC)]
        pieces += [(wo[:, 4 * i:4 * i + 4], wo_hi[:, 4 * i:4 * i + 4], wo_lo[:, 4 * i:4 * i + 4]) for i in range(2)]
        pieces += [(pw[:, i], pw_hi[:, i], pw_lo[:, i]) for i in range(WC)]
        NW, WO_AT = len(pieces), 2
        PIECE_AT = {0: (0,), 1: (1,), 3: (2,), 4: (3,), 6: (4,), 7: (5,)}

        def slot(i):
            st = stage[:, i % 2]
            return st.rearrange("p (a b) -> p a b", a=4) if len(pieces[i][0].shape) == 3 else st

        EXTRAS = {0: (("v", 3, -1, 1), ("y", 1, -2, 2)), 1: (("y", 2, -2, 0),), 2: (("y", 3, -2, 1),), 3: (("v", 0, 0, 2),),
                  4: (("v", 1, 0, 0),), 5: (("a", 0, -1, 1),), 6: (("a", 1, -1, 1),), 7: (("v", 2, 0, 2), ("y", 0, -1, 0))}

        def known(n):
            return isinstance(n, int)

        def live(n, end):
            return not known(n) or 0 <= n < end

        def groups(eng, step, start=None):
            def group(g, par):
                if start:
                    start(g, par)
                for i in range(NP):
                    step(g, i, par)
            group(0, 0)
            group(1, 1)
            with eng.Fori(1, NG // 2 - 1) as k:
                group(2 * k, 0)
                group(2 * k + 1, 1)
            for g in range(NG - 2, NG + 2):
                group(g, g % 2)

        def extras(g, i):
            for kind, n, rel, bank in EXTRAS[i]:
                if live(g + rel, NG):
                    yield kind, n, g + rel, bank, rel

        def vcols(n):
            return n % 2, slice(n // 2 * BANK, (n // 2 + 1) * BANK)

        def ycols(n):
            return n // 2, slice(n % 2 * BANK, (n % 2 + 1) * BANK)

        @block.sync
        def _(sync):
            def load_piece(i):
                wait(sync, s["w_lo_ready"], i - 1)
                if i >= WO_AT + 2:
                    sync.wait_ge(s["bvo_done"], 1)
                sync.dma_start(slot(i), pieces[i][0]).then_inc(w_loaded[i % 2], 16)

            def load_c(g):
                sync.dma_start(c_raw[:], c_dram[:, :, bass.ds(GT * g, GT)].rearrange("m p l -> p m l")).then_inc(s["c_loaded"], 16)

            def x_rows(t, g):
                return t[bass.ds(GT * g, GT), :].rearrange("(k p) d -> p k d", p=P)

            load_piece(0)
            load_piece(1)
            sync.wait_ge(c_stored, 16 * MC * N)
            sync.wait_ge(s["c0_lo_ready"], MC)
            load_c(1)
            sync.dma_start(pb_r[:], pb.to_broadcast([P, DM])).then_inc(s["pb_loaded"], 16)
            for i in range(2, NW):
                load_piece(i)
            sync.wait_ge(s["w_lo_ready"], NW)

            def start(g, par):
                if live(g - 2, NG):
                    sync.wait_ge(s["x1_ready"], YT * (g - 1))
                    sync.dma_start(x_rows(x1, g - 2), xr[:]).then_inc(x1_stored, 16)
                if live(g - 1, NG):
                    wait(sync, x1_stored, 16 * (g - 1))
                    sync.dma_start(xr[:], x_rows(x, g - 1)).then_inc(s["x_loaded"], 16)
                if live(g + 2, NG):
                    sync.wait_ge(s["c_lo_ready"], MC * (g + 1))
                    load_c(g + 2)

            groups(sync, lambda g, i, par: None, start)
            sync.wait_ge(x1_stored, 16 * (NG - 1))

        @block.gpsimd
        def _(pool):
            pool.memset(mask[:], 0.0).then_inc(s["mask0"], 1)
            pool.wait_ge(s["mask0"], 1)
            pool.affine_select(out=mask[:], in_=mask[:], compare_op=ALU.is_ge, fill=MASKED, base=0,
                               pattern=[[-1, P]], channel_multiplier=1).then_inc(s["mask_ready"], 1)
            pool.memset(k_hi[:].bitcast(F32), 0.0).then_inc(s["k_hi_zero"], 1)

            def c_sum(g, m):
                if m == 0:
                    pool.wait_ge(s["c_loaded"], 16 * g)
                pool.tensor_tensor(c_raw[:, m], c_raw[:, m], cb_c[:, m:m + 1].to_broadcast([P, GT]), ALU.add).then_inc(s["c_sum_ready"], 1)

            def c_low(g, par, m):
                pool.wait_ge(s["c_hi_ready"], MC * (g - 1) + m + 1)
                pool.tensor_tensor(c_lo[:, par, m], c_raw[:, m], c_hi[par][:, m], ALU.subtract).then_inc(s["c_lo_ready"], 1)

            def step(g, i, par):
                J = NP * g + i
                if live(J - NRM, NJ):
                    j4 = (i - NRM) % 4
                    pool.wait_ge(s["rrec_ready"], J - NRM + 1)
                    pool.tensor_tensor(pr[:, j4], pr[:, j4], rrec[:, j4].unsqueeze(2).to_broadcast([P, UN, P]), ALU.mult).then_inc(s["p_ready"], 1)
                if not (known(g) and g + 1 >= NG):
                    if i < MC:
                        c_sum(g + 1, i)
                    if i >= 2:
                        c_low(g + 1, 1 - par, i - 2)
                if i in (4, 5) and live(g - 1, NG):
                    if i == 4:
                        pool.wait_ge(s["x_loaded"], 16 * g)
                        if known(g) and g == 1:
                            pool.wait_ge(s["pb_loaded"], 16)
                    pool.tensor_tensor(xr[:, i - 4], xr[:, i - 4], pb_r[:], ALU.add).then_inc(s["xb_ready"], 1)

            groups(pool, step)

        @block.scalar
        def _(act):
            def piece(i):
                act.wait_ge(w_loaded[i % 2], 16 * (i // 2 + 1))
                act.activation(pieces[i][1], slot(i), ACT.Copy).then_inc(s["w_hi_ready"], 1)

            def c_high(g, par, m):
                act.wait_ge(s["c_sum_ready"], MC * (g - 1) + m + 1)
                act.activation(c_hi[par][:, m], c_raw[:, m], ACT.Copy).then_inc(s["c_hi_ready"], 1)

            act.wait_ge(s["k_hi_zero"], 1)

            def step(g, i, par):
                J = NP * g + i
                if live(J - OT, NJ):
                    j, opar = (i - OT) % NP, par if i >= OT else 1 - par
                    act.wait_ge(s["o_done"], J - OT + 1)
                    if j == 0 and live(g - 2, NG):
                        act.wait_ge(s["a_done"], WC * (g - 1))
                    for h in range(2):
                        e = slice(h * DH, (h + 1) * DH)
                        o = act.activation(oT_hi[e, opar, j].rearrange("p (b t) -> p b t", b=GB), op[e, :, h], ACT.Copy)
                    o.then_inc(s["oT_hi_ready"], 1)
                if live(J - TR, NJ):
                    act.wait_ge(s["pT_done"], J - TR + 1)
                    wait(act, s["o_done"], J - TR - 1)
                    act.activation(pT_hi[:, (i - TR) % 2], ptp[:], ACT.Copy).then_inc(s["pT_hi_ready"], 1)
                if live(J - SC, NJ):
                    j2, j4 = (i - SC) % 2, (i - SC) % 4
                    act.wait_ge(s["max_ready"], J - SC + 1)
                    wait(act, s["rrec_ready"], J - SC - 1)
                    for un in range(UN):
                        e = act.activation(pr[:, j4, un], pr[:, j4, un], ACT.Exp, bias=negmax[:, j2, un:un + 1], scale=-1.0,
                                           accum_out=rsum[:, j2, un:un + 1])
                    e.then_inc(s["exp_ready"], 1)
                if live(J, NJ):
                    act.wait_ge(s["qk_done"], J + 1)
                    wait(act, s["sc_done"], J - 1)
                    act.activation(q_hi[:, i % 2], qkp[:, i % 2, 0], ACT.Identity, bias=bqk_c[:, 0, i:i + 1])
                    for h in range(2):
                        e = slice(h * DH, (h + 1) * DH)
                        k = act.activation(k_hi[e, i % 2, :, h], qkp[e, i % 2, 1].rearrange("p (b t) -> p b t", b=GB), ACT.Identity, bias=bqk_c[e, 1, i:i + 1])
                    k.then_inc(s["qk_hi_ready"], 1)
                if not (known(g) and g + 1 >= NG) and 1 <= i <= MC:
                    c_high(g + 1, 1 - par, i - 1)
                for kind, n, eg, bank, _rel in extras(g, i):
                    if kind == "v":
                        act.wait_ge(s["v_done"], VT * eg + n + 1)
                        k, cols = vcols(n)
                        act.activation(v_hi[:, k, cols], gp[:, bank], ACT.Copy).then_inc(s["v_hi_ready"], 1)
                    if kind == "a" and n == WC - 1:
                        act.wait_ge(s["a_done"], WC * (eg + 1))
                        wait(act, s["y_done"], YT * eg)
                        for d in range(WC):
                            a = act.activation(a_hi[:, d], gp[:, bank, d * GT:(d + 1) * GT], ACT.Identity, bias=ba_c[:, d:d + 1])
                        a.then_inc(s["a_hi_ready"], 1)
                if known(g) and g == 0:
                    for n in PIECE_AT.get(i, ()):
                        piece(n)

            groups(act, step)

        @block.vector
        def _(dve):
            def piece(i):
                dve.wait_ge(s["w_hi_ready"], i + 1)
                dve.tensor_tensor(pieces[i][2], slot(i), pieces[i][1], ALU.subtract).then_inc(s["w_lo_ready"], 1)

            def low(out, src, bias, hi):
                return dve.scalar_tensor_tensor(out, src, bias, hi, ALU.add, ALU.subtract)

            for m in range(MC):
                dve.tensor_tensor(c_lo[:, 0, m], c_raw[:, m], c0_hi[:, m], ALU.subtract).then_inc(s["c0_lo_ready"], 1)
            dve.memset(k_lo[:].bitcast(F32), 0.0).then_inc(s["k_lo_zero"], 1)
            dve.wait_ge(s["mask_ready"], 1)
            dve.wait_ge(s["k_lo_zero"], 1)

            def step(g, i, par):
                J = NP * g + i
                if live(J - SC, NJ):
                    dve.wait_ge(s["sc_done"], J - SC + 1)
                    wait(dve, s["pT_done"], J - SC - 3)
                if live(J - NRM, NJ):
                    dve.wait_ge(s["exp_ready"], J - NRM + 1)
                    wait(dve, s["p_ready"], J - NRM - 3)
                    dve.reciprocal(rrec[:, (i - NRM) % 4], rsum[:, (i - NRM) % 2]).then_inc(s["rrec_ready"], 1)
                if live(J - SC, NJ):
                    j2, j4 = (i - SC) % 2, (i - SC) % 4
                    for un in range(UN):
                        b, h = un // 2, un % 2
                        m = dve.tensor_tensor_reduce(out=pr[:, j4, un], in0=scp[:, b, h * P:(h + 1) * P], in1=mask[:], scale=-DH ** -0.5,
                                                     scalar=-MASKED, op0=ALU.add, op1=ALU.min, accum_out=negmax[:, j2, un:un + 1])
                    m.then_inc(s["max_ready"], 1)
                if live(J - OT, NJ):
                    j, opar = (i - OT) % NP, par if i >= OT else 1 - par
                    dve.wait_ge(s["oT_hi_ready"], J - OT + 1)
                    for h in range(2):
                        e = slice(h * DH, (h + 1) * DH)
                        hi, lo = (t[e, opar, j].rearrange("p (b t) -> p b t", b=GB) for t in (oT_hi, oT_lo))
                        o = dve.tensor_tensor(lo, op[e, :, h], hi, ALU.subtract)
                    o.then_inc(s["oT_lo_ready"], 1)
                if live(J - TR, NJ):
                    dve.wait_ge(s["pT_hi_ready"], J - TR + 1)
                    dve.tensor_tensor(pT_lo[:, (i - TR) % 2], ptp[:], pT_hi[:, (i - TR) % 2], ALU.subtract).then_inc(s["pT_lo_ready"], 1)
                if live(J, NJ):
                    dve.wait_ge(s["qk_hi_ready"], J + 1)
                    low(q_lo[:, i % 2], qkp[:, i % 2, 0], bqk_c[:, 0, i:i + 1], q_hi[:, i % 2])
                    for h in range(2):
                        e = slice(h * DH, (h + 1) * DH)
                        k = low(k_lo[e, i % 2, :, h], qkp[e, i % 2, 1].rearrange("p (b t) -> p b t", b=GB), bqk_c[e, 1, i:i + 1], k_hi[e, i % 2, :, h])
                    k.then_inc(s["qk_lo_ready"], 1)
                for kind, n, eg, bank, _rel in extras(g, i):
                    if kind == "v":
                        dve.wait_ge(s["v_hi_ready"], VT * eg + n + 1)
                        k, cols = vcols(n)
                        dve.tensor_tensor(v_lo[:, k, cols], gp[:, bank], v_hi[:, k, cols], ALU.subtract).then_inc(s["v_lo_ready"], 1)
                    if kind == "a" and n == WC - 1:
                        dve.wait_ge(s["a_hi_ready"], eg + 1)
                        for d in range(WC):
                            a = low(a_lo[:, d], gp[:, bank, d * GT:(d + 1) * GT], ba_c[:, d:d + 1], a_hi[:, d])
                        a.then_inc(s["a_lo_ready"], 1)
                    if kind == "y":
                        dve.wait_ge(s["y_done"], YT * eg + n + 1)
                        if n == 0:
                            dve.wait_ge(s["xb_ready"], GB * (eg + 1))
                        k, cols = ycols(n)
                        dve.tensor_tensor(xr[:, k, cols], gp[:, bank], xr[:, k, cols], ALU.add).then_inc(s["x1_ready"], 1)
                if known(g) and g == 0:
                    for n in PIECE_AT.get(i, ()):
                        piece(n)
                    if i == 6:
                        dve.wait_ge(s["bvo_done"], 1)
                        dve.tensor_tensor(ba_c[:], gp[:, 1, 0:WC], bo_c[:], ALU.add).then_inc(s["ba_ready"], 1)

            groups(dve, step)

        @block.tensor
        def _(pe):
            def setup_bias():
                for i in range(2):
                    pe.wait_ge(w_loaded[(WO_AT + i) % 2], 16 * ((WO_AT + i) // 2 + 1))
                for d in range(WC):
                    for c in range(OC):
                        raw = slot(WO_AT + c // 4)
                        mm = pe.matmul(gp[:, 1, d:d + 1], raw[:, c % 4, d * P:(d + 1) * P], bv_c[:, c:c + 1], start=(c == 0), stop=(c == OC - 1))
                mm.then_inc(s["bvo_done"], 1)

            def extra(kind, n, eg, bank, par):
                if kind == "v":
                    if n == 0:
                        wait(pe, s["x1_ready"], YT * (eg - 2) + 2)
                    elif n == 1:
                        wait(pe, s["x1_ready"], YT * (eg - 2) + 3)
                    elif n == 2:
                        pe.wait_ge(s["v_lo_ready"], VT * eg + 1)
                    elif known(eg) and eg == 0:
                        pe.wait_ge(s["ba_ready"], 1)
                    else:
                        pe.wait_ge(s["a_lo_ready"], eg)
                    k, cols = vcols(n)
                    t = slice(k * P, (k + 1) * P)
                    for c in range(WC):
                        mm = three_pass(pe, gp[:, bank], c_hi[par][:, 2 * WC + c, t], c_lo[:, par, 2 * WC + c, t],
                                        wv_hi[:, c, cols], wv_lo[:, c, cols], c == 0, c == WC - 1)
                    mm.then_inc(s["v_done"], 1)
                if kind == "a":
                    if n == 0:
                        wait(pe, s["x1_ready"], YT * eg)
                        pe.wait_ge(s["oT_lo_ready"], NP * (eg + 1) - 1)
                    for c in range(OC):
                        if n == 0 and c == OC - 1:
                            pe.wait_ge(s["oT_lo_ready"], NP * (eg + 1))
                        mm = three_pass(pe, gp[:, bank, n * GT:(n + 1) * GT], wo_hi[:, c, n * P:(n + 1) * P], wo_lo[:, c, n * P:(n + 1) * P],
                                        oT_hi[:, par, c], oT_lo[:, par, c], c == 0, c == OC - 1)
                    mm.then_inc(s["a_done"], 1)
                if kind == "y":
                    if n == 0:
                        pe.wait_ge(s["a_lo_ready"], eg + 1)
                        if live(eg + 1, NG):
                            pe.wait_ge(s["v_lo_ready"], VT * (eg + 1) + 2)
                    elif n == 1 and live(eg + 1, NG):
                        pe.wait_ge(s["v_lo_ready"], VT * (eg + 1) + 3)
                    elif n == 2:
                        pe.wait_ge(s["x1_ready"], YT * eg + 1)
                    elif n == 3 and live(eg + 1, NG):
                        pe.wait_ge(s["v_lo_ready"], VT * (eg + 1) + 4)
                    k, cols = ycols(n)
                    t = slice(k * P, (k + 1) * P)
                    for c in range(WC):
                        mm = three_pass(pe, gp[:, bank], a_hi[:, c, t], a_lo[:, c, t], pw_hi[:, c, cols], pw_lo[:, c, cols], c == 0, c == WC - 1)
                    mm.then_inc(s["y_done"], 1)

            def step(g, i, par):
                J = NP * g + i
                if known(g) and g == 0:
                    if i == 3:
                        pe.wait_ge(s["c0_lo_ready"], MC)
                        pe.wait_ge(s["w_lo_ready"], WO_AT)
                    if i == 5:
                        setup_bias()
                if known(g) and g == 1 and i == 4:
                    pe.wait_ge(s["w_lo_ready"], NW)
                if live(J - SC, NJ):
                    j2 = (i - SC) % 2
                    pe.wait_ge(s["qk_lo_ready"], J - SC + 1)
                    wait(pe, s["max_ready"], J - SC)
                    for b in range(GB):
                        t = slice(b * P, (b + 1) * P)
                        mm = three_pass(pe, scp[:, b], q_hi[:, j2, t], q_lo[:, j2, t], k_hi[:, j2, b].rearrange("p h t -> p (h t)"),
                                        k_lo[:, j2, b].rearrange("p h t -> p (h t)"), True, True)
                    mm.then_inc(s["sc_done"], 1)
                if live(J - TR, NJ):
                    pe.wait_ge(s["p_ready"], J - TR + 1)
                    wait(pe, s["pT_lo_ready"], J - TR)
                    for un in range(UN):
                        b, h = un // 2, un % 2
                        mm = pe.transpose(ptp[:, b, h * P:(h + 1) * P], pr[:, (i - TR) % 4, un], ident[:])
                    mm.then_inc(s["pT_done"], 1)
                if live(J, NJ):
                    if i == 0 and not (known(g) and g == 0):
                        pe.wait_ge(s["c_lo_ready"], MC * g)
                    wait(pe, s["qk_lo_ready"], J - 1)
                    for k in range(2):
                        for c in range(WC):
                            if known(J) and J == 0:
                                pe.wait_ge(s["c0_lo_ready"], WC * k + c + 1)
                            mm = three_pass(pe, qkp[:, i % 2, k], wqk_hi[:, k, c, i * P:(i + 1) * P], wqk_lo[:, k, c, i * P:(i + 1) * P],
                                            c_hi[par][:, WC * k + c], c_lo[:, par, WC * k + c], c == 0, c == WC - 1)
                    mm.then_inc(s["qk_done"], 1)
                for kind, n, eg, bank, rel in extras(g, i):
                    extra(kind, n, eg, bank, (par + rel) % 2)
                if live(J - PV, NJ):
                    j, j2 = (i - PV) % NP, (i - PV) % 2
                    pe.wait_ge(s["pT_lo_ready"], J - PV + 1)
                    wait(pe, s["oT_lo_ready"], J - PV)
                    if j == 0:
                        pe.wait_ge(s["v_lo_ready"], VT * g + 2)
                    if j == NP // 2:
                        pe.wait_ge(s["v_lo_ready"], VT * g)
                    for b in range(GB):
                        mm = three_pass(pe, op[:, b].rearrange("p h t -> p (h t)"), v_hi[:, b, j * P:(j + 1) * P], v_lo[:, b, j * P:(j + 1) * P],
                                        pT_hi[:, j2, b], pT_lo[:, j2, b], True, True)
                    mm.then_inc(s["o_done"], 1)

            groups(pe, step)


def ffn_phase(nc, x1, x1_stored, w_base, b_base, lora_a, lora_b, router_w, router_b, prior, active, out, ident):
    TT = TOK // P
    NH = DM // BANK
    Z = ER + E_ACT
    with ExitStack() as ctx:
        sp = Space(nc, ctx, "ffn")
        w_raw = sp.sb("w_raw", [P, 2, 2, DM])
        w_hi = sp.sb("w_hi", [P, DC, DM], F32R)
        w_lo = sp.sb("w_lo", [P, DC, DM], F32R)
        a_raw = sp.sb("a_raw", [P, DC, ER])
        r_raw = sp.sb("r_raw", [P, E_ACT, DC])
        az_hi = sp.sb("az_hi", [P, DC, Z], F32R)
        az_lo = sp.sb("az_lo", [P, DC, Z], F32R)
        act_sb = sp.sb("active", [1, E_ACT], I32)
        b_raw = sp.sb("b_raw", [ER + 1, DM])
        b_hi = sp.sb("b_hi", [ER + 1, DM], F32R)
        b_lo = sp.sb("b_lo", [ER + 1, DM], F32R)
        KB = 3 * ER + 2
        b_stack = sp.sb("b_stack", [KB, DM], F32R)
        lbias = sp.sb("lbias", [P, 2, E_ACT])
        logp = sp.sb("logp", [P, E_ACT])
        lsum = sp.sb("lsum", [P, E_ACT])
        x1t = sp.sb("x1t", [P, 4, DM])
        xn = sp.sb("xn", [P, 2, DM])
        xT_hi = sp.sb("xT_hi", [P, 2, DC, P], F32R)
        xT_lo = sp.sb("xT_lo", [P, 2, DC, P], F32R)
        y = sp.sb("y", [P, 2, DM])
        stats = sp.sb("stats", [P, 2, 2, 6])
        mv = sp.sb("mv", [P, 2, 2])
        vareps = sp.sb("vareps", [P, 2, 1])
        rstd = sp.sb("rstd", [P, 2, 1])
        mhalf = sp.sb("mhalf", [P, 1])
        logit = sp.sb("logit", [P, E_ACT])
        negmax = sp.sb("negmax", [P, 1])
        expl = sp.sb("expl", [P, E_ACT])
        esum = sp.sb("esum", [P, 1])
        erec = sp.sb("erec", [P, 1])
        alpha = sp.sb("alpha", [P, E_ACT])
        az = sp.sb("az", [P, ER])
        azs = sp.sb("azs", [P, 2, KB], F32R)
        azsT = sp.sb("azsT", [KB, 2, P], F32R)

        tp = sp.ps("tp", [P, 2, BANK])
        zp = sp.ps("zp", [P, BANK])
        ap = sp.ps("ap", [P, BANK])
        yp = sp.ps("yp", [P, 2, NH, BANK])

        names = ("active_loaded", "az_loaded", "b_loaded", "lbias_loaded", "az_split_hi", "az_split_lo", "b_split_hi", "b_split_lo", "b_stacked",
                 "w_hi_ready", "w_lo_ready", "logp_in", "logp_ready", "lsum_ready", "ones_ready", "power_ready",
                 "stats_done", "mv_done", "var_ready", "rstd_ready", "xn_ready", "transposed", "xT_hi_ready", "xT_lo_ready",
                 "z_done", "logit_ready", "max_ready", "exp_ready", "rec_ready", "alpha_ready", "az_ready", "azs_hi_ready", "azs_ready",
                 "azT_done", "azsT_ready", "y_done", "y_ready")
        s = {n: sp.sem(n) for n in names}
        w_loaded = [sp.sem(f"w_loaded{i}") for i in range(2)]
        x_loaded = [sp.sem(f"x_loaded{i}") for i in range(4)]
        y_stored = [sp.sem(f"y_stored{i}") for i in range(2)]
        block = ctx.enter_context(nc.Block())

        def tiles(eng, one_tile, lo=0):
            for q in range(4):
                one_tile(q, q)
            with eng.Fori(1, TT // 4 - 1) as k:
                for q in range(4):
                    one_tile(4 * k + q, q)
            for q in range(4):
                one_tile(TT - 4 + q, q)

        def is_last(t):
            return isinstance(t, int) and t == TT - 1

        @block.sync
        def _(sync):
            sync.dma_start(act_sb[:], active).then_inc(s["active_loaded"], 16)

            def load(t, q):
                wait(sync, s["y_ready"], NH * (t - 3))
                sync.dma_start(x1t[:, q], x1[bass.ds(t * P, P)]).then_inc(x_loaded[q], 16)

            load(0, 0)
            for i in range(DC // 2):
                wait(sync, s["w_lo_ready"], i - 1)
                sync.dma_start(w_raw[:, i % 2], w_base[:, 2 * i:2 * i + 2]).then_inc(w_loaded[i % 2], 16)
                if i == 0:
                    sync.wait_ge(s["active_loaded"], 16)
                    for e in range(E_ACT):
                        expert = sync.value_load(act_sb[0:1, e:e + 1], min_val=0, max_val=E_TOT - 1)
                        sync.dma_start(a_raw[:, :, e * RANK:(e + 1) * RANK], lora_a[bass.ds(expert, 1)].rearrange("e p c r -> (e p) c r")).then_inc(s["az_loaded"], 16)
                        sync.dma_start(r_raw[:, e], router_w[bass.ds(expert, 1)].rearrange("e p c -> (e p) c")).then_inc(s["az_loaded"], 16)
                        sync.dma_start(b_raw[e * RANK:(e + 1) * RANK, :], lora_b[bass.ds(expert, 1)].rearrange("e r o -> (e r) o")).then_inc(s["b_loaded"], 16)
                        sync.dma_start(lbias[:, 0, e:e + 1], router_b[bass.ds(expert, 1), :].to_broadcast([P, 1])).then_inc(s["lbias_loaded"], 16)
                        sync.dma_start(lbias[:, 1, e:e + 1], prior[bass.ds(expert, 1), :].to_broadcast([P, 1])).then_inc(s["lbias_loaded"], 16)
                    sync.dma_start(b_raw[ER:ER + 1, :], b_base).then_inc(s["b_loaded"], 16)
                if i == 1:
                    for t in range(1, 4):
                        load(t, t)
            sync.wait_ge(s["b_split_lo"], 1)
            for n, (part, r0, r1, at) in enumerate(((b_hi, 0, ER, 0), (b_hi, 0, ER, ER), (b_lo, 0, ER, 2 * ER),
                                                    (b_hi, ER, ER + 1, 3 * ER), (b_lo, ER, ER + 1, 3 * ER + 1))):
                sync.dma_start(b_stack[at:at + r1 - r0, :].bitcast(F32), part[r0:r1, :].bitcast(F32)).then_inc(s["b_stacked"], 16)

            def later(t, q):
                if not (isinstance(t, int) and t < 4):
                    load(t, q)

            sync.wait_ge(x1_stored, 16 * (TOK // GT))
            tiles(sync, later)

        @block.gpsimd
        def _(pool):
            pool.memset(mhalf[:], -0.5).then_inc(s["power_ready"], 1)
            pool.wait_ge(s["power_ready"], 1)

            def power(t, q):
                pool.wait_ge(s["var_ready"], t + 1)
                pool.tensor_tensor(rstd[:, q % 2], vareps[:, q % 2], mhalf[:], ALU.pow).then_inc(s["rstd_ready"], 1)

            def store(t, q):
                pool.wait_ge(s["y_ready"], NH * (t + 1))
                pool.dma_start(out[bass.ds(t * P, P)], y[:, q % 2]).then_inc(y_stored[q % 2], 16)

            def tile(t, q):
                if isinstance(t, int) and t == 0:
                    power(0, 0)
                if not is_last(t):
                    power(t + 1, (q + 1) % 4)
                store(t, q)

            tiles(pool, tile)
            for par in range(2):
                pool.wait_ge(y_stored[par], 16 * (TT // 2))

        @block.scalar
        def _(act):
            act.wait_ge(s["logp_in"], 1)
            act.activation(logp[:], lbias[:, 1], ACT.Ln).then_inc(s["logp_ready"], 1)

            def xT(t, q):
                for h in range(2):
                    act.wait_ge(s["transposed"], 2 * t + h + 1)
                    if h == 0:
                        wait(act, s["y_done"], NH * (t - 1))
                    act.activation(xT_hi[:, q % 2, 4 * h:4 * h + 4], tp[:, h], ACT.Copy).then_inc(s["xT_hi_ready"], 1)

            xT(0, 0)
            act.wait_ge(s["az_loaded"], 32 * E_ACT)
            act.activation(az_hi[:, :, 0:ER], a_raw[:], ACT.Copy)
            act.activation(az_hi[:, :, ER:Z], r_raw[:].rearrange("p e c -> p c e"), ACT.Copy).then_inc(s["az_split_hi"], 1)
            for i in range(DC // 2):
                act.wait_ge(w_loaded[i % 2], 16 * (i // 2 + 1))
                act.activation(w_hi[:, 2 * i:2 * i + 2], w_raw[:, i % 2], ACT.Copy).then_inc(s["w_hi_ready"], 1)
                if i == 1:
                    act.wait_ge(s["b_loaded"], 16 * (E_ACT + 1))
                    act.activation(b_hi[:], b_raw[:], ACT.Copy).then_inc(s["b_split_hi"], 1)

            def tile(t, q):
                act.wait_ge(s["max_ready"], t + 1)
                act.activation(expl[:], logit[:], ACT.Exp, bias=negmax[:], accum_out=esum[:]).then_inc(s["exp_ready"], 1)
                act.wait_ge(s["azT_done"], t + 1)
                wait(act, s["y_done"], NH * (t - 1))
                act.activation(azsT[:, q % 2], ap[0:KB, 0:P], ACT.Copy).then_inc(s["azsT_ready"], 1)
                if not is_last(t):
                    xT(t + 1, (q + 1) % 4)

            tiles(act, tile)

        @block.vector
        def _(dve):
            def statistics(t, q):
                par = q % 2
                dve.wait_ge(x_loaded[q], 16 * ((t - q) // 4 + 1) if isinstance(t, int) else 4 * (t - q) + 16)
                wait(dve, s["mv_done"], t - 1)
                dve.bn_stats(stats[:, par, 0], x1t[:, q, 0:DM // 2])
                dve.bn_stats(stats[:, par, 1], x1t[:, q, DM // 2:DM]).then_inc(s["stats_done"], 1)

            def variance(t, q):
                par = q % 2
                dve.bn_aggr(mv[:, par], stats[:, par]).then_inc(s["mv_done"], 1)
                dve.wait_ge(s["mv_done"], t + 1)
                dve.tensor_scalar(vareps[:, par], mv[:, par, 1:2], EPS, None, ALU.add).then_inc(s["var_ready"], 1)

            def scale(t, q):
                par = q % 2
                dve.wait_ge(s["rstd_ready"], t + 1)
                wait(dve, s["transposed"], 2 * (t - 1))
                dve.tensor_scalar(xn[:, par], x1t[:, q], mv[:, par, 0:1], rstd[:, par], ALU.subtract, ALU.mult).then_inc(s["xn_ready"], 1)

            def xT_low(t, q):
                for h in range(2):
                    dve.wait_ge(s["xT_hi_ready"], 2 * t + h + 1)
                    dve.tensor_tensor(xT_lo[:, q % 2, 4 * h:4 * h + 4], tp[:, h], xT_hi[:, q % 2, 4 * h:4 * h + 4], ALU.subtract).then_inc(s["xT_lo_ready"], 1)

            def gate(t, q):
                par = q % 2
                if not is_last(t):
                    dve.wait_ge(s["stats_done"], t + 2)
                dve.wait_ge(s["z_done"], t + 1)
                wait(dve, s["exp_ready"], t)
                dve.tensor_tensor(logit[:], zp[:, ER:Z], lsum[:], ALU.add).then_inc(s["logit_ready"], 1)
                if not is_last(t):
                    variance(t + 1, (q + 1) % 4)
                dve.wait_ge(s["logit_ready"], t + 1)
                dve.tensor_reduce(negmax[:], logit[:], AX_X, ALU.max, negate=True).then_inc(s["max_ready"], 1)
                dve.wait_ge(s["exp_ready"], t + 1)
                dve.reciprocal(erec[:], esum[:]).then_inc(s["rec_ready"], 1)
                dve.wait_ge(s["rec_ready"], t + 1)
                dve.tensor_scalar(alpha[:], expl[:], erec[:], LORA_SCALE, ALU.mult, ALU.mult).then_inc(s["alpha_ready"], 1)
                dve.wait_ge(s["alpha_ready"], t + 1)
                dve.tensor_tensor(az[:].rearrange("p (e r) -> p e r", r=RANK), zp[:, 0:ER].rearrange("p (e r) -> p e r", r=RANK),
                                  alpha[:].unsqueeze(2).to_broadcast([P, E_ACT, RANK]), ALU.mult).then_inc(s["az_ready"], 1)
                dve.wait_ge(s["az_ready"], t + 1)
                wait(dve, s["azT_done"], t - 1)
                dve.tensor_copy(azs[:, par, 0:ER], az[:]).then_inc(s["azs_hi_ready"], 1)
                dve.tensor_copy(azs[:, par, 2 * ER:3 * ER], az[:])
                dve.wait_ge(s["azs_hi_ready"], t + 1)
                dve.tensor_tensor(azs[:, par, ER:2 * ER], az[:], azs[:, par, 0:ER], ALU.subtract).then_inc(s["azs_ready"], 1)

            def outputs(t, q, h):
                dve.wait_ge(s["y_done"], NH * t + h + 1)
                if h == 0:
                    if isinstance(t, int):
                        wait(dve, y_stored[q % 2], 16 * (t // 2))
                    else:
                        dve.wait_ge(y_stored[q % 2], 8 * (t - q % 2))
                dve.tensor_tensor(y[:, q % 2, h * BANK:(h + 1) * BANK], yp[:, q % 2, h], x1t[:, q, h * BANK:(h + 1) * BANK], ALU.add).then_inc(s["y_ready"], 1)

            dve.memset(azs[:, :, 3 * ER:KB].bitcast(F32), 1.0).then_inc(s["ones_ready"], 1)
            statistics(0, 0)
            dve.wait_ge(s["stats_done"], 1)
            variance(0, 0)
            scale(0, 0)
            dve.wait_ge(s["lbias_loaded"], 32 * E_ACT)
            dve.tensor_scalar(lbias[:, 1], lbias[:, 1], PRIOR_EPS, None, ALU.add).then_inc(s["logp_in"], 1)
            xT_low(0, 0)
            dve.wait_ge(s["logp_ready"], 1)
            dve.tensor_tensor(lsum[:], logp[:], lbias[:, 0], ALU.add).then_inc(s["lsum_ready"], 1)
            dve.wait_ge(s["az_split_hi"], 1)
            dve.tensor_tensor(az_lo[:, :, 0:ER], a_raw[:], az_hi[:, :, 0:ER], ALU.subtract)
            dve.tensor_tensor(az_lo[:, :, ER:Z], r_raw[:].rearrange("p e c -> p c e"), az_hi[:, :, ER:Z], ALU.subtract).then_inc(s["az_split_lo"], 1)
            for i in range(DC // 2):
                dve.wait_ge(s["w_hi_ready"], i + 1)
                dve.tensor_tensor(w_lo[:, 2 * i:2 * i + 2], w_raw[:, i % 2], w_hi[:, 2 * i:2 * i + 2], ALU.subtract).then_inc(s["w_lo_ready"], 1)
                if i == 1:
                    dve.wait_ge(s["b_split_hi"], 1)
                    dve.tensor_tensor(b_lo[:], b_raw[:], b_hi[:], ALU.subtract).then_inc(s["b_split_lo"], 1)
            dve.wait_ge(s["lsum_ready"], 1)

            def tile(t, q):
                if not is_last(t):
                    statistics(t + 1, (q + 1) % 4)
                gate(t, q)
                if not is_last(t):
                    scale(t + 1, (q + 1) % 4)
                    xT_low(t + 1, (q + 1) % 4)
                for h in range(NH):
                    outputs(t, q, h)

            tiles(dve, tile)

        @block.tensor
        def _(pe):
            def transposes(t, q):
                pe.wait_ge(s["xn_ready"], t + 1)
                for h in range(2):
                    wait(pe, s["xT_lo_ready"], 2 * (t - 1) + h + 1)
                    for c in range(4 * h, 4 * h + 4):
                        tr = pe.transpose(tp[:, h, (c % 4) * P:(c % 4 + 1) * P], xn[:, q % 2, c * P:(c + 1) * P], ident[:])
                    tr.then_inc(s["transposed"], 1)

            def dense(t, q, h):
                if h == 0:
                    wait(pe, s["y_ready"], NH * (t - 1))
                for c in range(DC):
                    if isinstance(t, int) and t == 0 and h == 0 and c % 2 == 0:
                        pe.wait_ge(s["w_lo_ready"], c // 2 + 1)
                    three_pass(pe, yp[:, q % 2, h], xT_hi[:, q % 2, c], xT_lo[:, q % 2, c],
                               w_hi[:, c, h * BANK:(h + 1) * BANK], w_lo[:, c, h * BANK:(h + 1) * BANK], c == 0, False)

            def tile(t, q):
                if isinstance(t, int) and t == 0:
                    transposes(0, 0)
                    pe.wait_ge(s["az_split_lo"], 1)
                pe.wait_ge(s["xT_lo_ready"], 2 * (t + 1))
                wait(pe, s["az_ready"], t)
                for c in range(DC):
                    z = three_pass(pe, zp[:, 0:Z], xT_hi[:, q % 2, c], xT_lo[:, q % 2, c], az_hi[:, c], az_lo[:, c], c == 0, c == DC - 1)
                z.then_inc(s["z_done"], 1)
                dense(t, q, 0)
                if isinstance(t, int) and t == 0:
                    pe.wait_ge(s["ones_ready"], 1)
                    pe.wait_ge(s["b_stacked"], 16 * 5)
                pe.wait_ge(s["azs_ready"], t + 1)
                wait(pe, s["azsT_ready"], t)
                pe.transpose(ap[0:KB, 0:P], azs[:, q % 2].bitcast(F32), ident[:]).then_inc(s["azT_done"], 1)
                if not is_last(t):
                    transposes(t + 1, (q + 1) % 4)
                dense(t, q, 1)
                pe.wait_ge(s["azsT_ready"], t + 1)
                for h in range(NH):
                    pe.matmul(yp[:, q % 2, h], azsT[:, q % 2], b_stack[:, h * BANK:(h + 1) * BANK], start=False, stop=True).then_inc(s["y_done"], 1)

            tiles(pe, tile)


def program(nc, x, conv_w, conv_b, wq, wk, wv, wo, pw, bq, bk, bv, bo, pb, w_base, b_base, lora_a, lora_b, router_w, router_b,
            prior, active, c_dram, x1_dram, out):
    with nc.sbuf_tensor("ident", [P, P], F32) as ident, ExitStack() as phases:
        with nc.semaphore("ident_zero") as ident_zero, nc.semaphore("ident_ready") as ident_ready, nc.Block() as block:
            @block.gpsimd
            def _(pool):
                pool.memset(ident[:], 0.0).then_inc(ident_zero, 1)
                pool.wait_ge(ident_zero, 1)
                pool.affine_select(out=ident[:], in_=ident[:], compare_op=ALU.not_equal, fill=1.0, base=0,
                                   pattern=[[-1, P]], channel_multiplier=1).then_inc(ident_ready, 1)
                pool.wait_ge(ident_ready, 1)
        flat = lambda t: t.rearrange("n l d -> (n l) d")
        offset = nc.sbuf_base
        x1_stored = phases.enter_context(nc.semaphore("x1_stored"))
        with nc.sbuf_tensor("shared", [P, SharedArea.SIZE], F32), nc.semaphore("c_stored") as c_stored:
            shared = SharedArea(nc, offset)
            conv_phase(nc, x, conv_w, c_dram, c_stored, ident, shared, wq, wk, conv_b, bq, bk, bv, bo)
            attention_phase(nc, flat(x), c_dram, c_stored, wv, wo, pw, pb, flat(x1_dram), x1_stored, ident, shared)
        ffn_phase(nc, flat(x1_dram), x1_stored, w_base, b_base, lora_a, lora_b, router_w, router_b, prior, active,
                  flat(out), ident)


def kernel(**inputs):
    import numpy as np
    import concourse.bacc as bacc
    from concourse.bass_utils import run_bass_kernel_spmd

    attn = {k[len("L0_attn_"):]: np.asarray(v) for k, v in inputs.items() if k.startswith("L0_attn_")}
    ffn = {k[len("L0_ffn_"):]: np.asarray(v) for k, v in inputs.items() if k.startswith("L0_ffn_")}
    rows = lambda a: a.reshape(-1, P, a.shape[-1]).transpose(1, 0, 2)
    column = lambda a: a.reshape(-1, P).T
    laid_out = {
        "x": attn["inputs"],
        "conv_w": attn["conv_w"].reshape(3, DC, P, MC, P).transpose(3, 2, 1, 0, 4),
        "conv_b": column(attn["conv_b"]),
        "wq": rows(attn["wq"].reshape(W, HW_)), "wk": rows(attn["wk"].reshape(W, HW_)), "wv": rows(attn["wv"].reshape(W, HW_)),
        "wo": rows(attn["wo"].reshape(HW_, W)), "pw": rows(attn["proj_w"]),
        "bq": column(attn["bq"]), "bk": column(attn["bk"]), "bv": column(attn["bv"]), "bo": column(attn["bo"]),
        "pb": attn["proj_b"].reshape(1, DM),
        "w_base": rows(ffn["W_base"].T), "b_base": ffn["b_base"].reshape(1, DM),
        "lora_a": ffn["lora_A"].reshape(E_TOT, RANK, DC, P).transpose(0, 3, 2, 1),
        "lora_b": ffn["lora_B"].transpose(0, 2, 1),
        "router_w": ffn["router_W"].reshape(E_TOT, DC, P).transpose(0, 2, 1),
        "router_b": ffn["router_b"].reshape(E_TOT, 1), "prior": ffn["domain_prior"].reshape(E_TOT, 1),
        "active": ffn["active"].reshape(1, E_ACT),
    }
    nc = bacc.Bacc("TRN2", target_bir_lowering=False, num_devices=1)
    arrays, args = {}, []
    for name, a in laid_out.items():
        a = np.ascontiguousarray(a)
        arrays[f"in_{name}"] = a
        args.append(nc.dram_tensor(f"in_{name}", a.shape, mybir.dt.from_np(a.dtype), kind="ExternalInput").ap())
    c_dram = nc.dram_tensor("c_scratch", (MC, P, TOK), F32, kind="Internal").ap()
    x1_dram = nc.dram_tensor("x1_scratch", (N, L, DM), F32, kind="Internal").ap()
    out = nc.dram_tensor("out_0", (N, L, DM), F32, kind="ExternalOutput").ap()
    program(nc, *args, c_dram, x1_dram, out)
    return run_bass_kernel_spmd(nc, [arrays], core_ids=[0]).results[0]["out_0"]
```
